# Optimizing a Trainium2 kernel written in Bass

```python
import numpy as np
import jax
import jax.numpy as jnp

def _softmax(x, axis=-1):
    return jax.nn.softmax(x, axis=axis)

def _gelu(x):
    return jax.nn.gelu(x, approximate=True)

def _silu(x):
    return jax.nn.silu(x)

def _sigmoid(x):
    return jax.nn.sigmoid(x)

def _layernorm(x, axis=-1, eps=1e-05):
    m = jnp.mean(x, axis=axis, keepdims=True)
    v = jnp.var(x, axis=axis, keepdims=True)
    return (x - m) / jnp.sqrt(v + eps)

def _scatter_add(tgt, idx, src, axis=0):
    return tgt.at[idx].add(src)

def _segment_sum(src, seg, n):
    return jax.ops.segment_sum(src, seg, n)
kernel_name = 'mk_gnn_resnorm_d4_gnn_r32_996065'

def setup_inputs(seed: int=0):
    np.random.seed(seed)
    _w = jnp.asarray

    def _rec_inputs():
        import jax
        import jax.numpy as jnp
        _gk = jax.random.key(seed)
        x = -0.0009044 + 1 * jax.random.normal(jax.random.fold_in(_gk, 1), (3125, 16), jnp.float32)
        _s = jax.random.randint(jax.random.fold_in(_gk, 2), (50000,), 0, 3125, jnp.int32)
        _d = jax.random.randint(jax.random.fold_in(_gk, 3), (50000,), 0, 3125, jnp.int32)
        _loop = jnp.arange(3125, dtype=jnp.int32)
        src = jnp.concatenate([_s, _d, _loop])
        dst = jnp.concatenate([_d, _s, _loop])
        _o = jnp.argsort(dst, stable=True)
        src = src[_o]
        dst = dst[_o]
        edge_attr_16 = -3.57403e-05 + 0.999761 * jax.random.normal(jax.random.fold_in(_gk, 12), (103125, 16), jnp.float32)
        edge_attr_6 = jax.random.uniform(jax.random.fold_in(_gk, 13), (103125, 6), jnp.float32, 0.0, 1)
        edge_type_8 = jax.random.randint(jax.random.fold_in(_gk, 15), (103125,), 0, 8, jnp.int32)
        return (x, src, dst, edge_attr_16, edge_attr_6, edge_type_8)
    x, src, dst, edge_attr_16, edge_attr_6, edge_type_8 = _rec_inputs()

    def _L0_gnn_setup():
        import jax, jax.numpy as jnp
        import numpy as np
        N = 3125
        E = 100000
        N_CHANNEL = 16

        def _init_linear(key, fan_in, fan_out):
            bound = 1.0 / np.sqrt(fan_in)
            kw, kb = jax.random.split(key)
            W = jax.random.uniform(kw, (fan_in, fan_out), jnp.float32, -bound, bound)
            b = jax.random.uniform(kb, (fan_out,), jnp.float32, -bound, bound)
            return (W, b)

        def gcn_conv(x, W, b, src, dst, n):
            h = x @ W
            loop = jnp.arange(n, dtype=src.dtype)
            s = jnp.concatenate([src, loop])
            d = jnp.concatenate([dst, loop])
            deg = jax.ops.segment_sum(jnp.ones_like(s, dtype=h.dtype), d, num_segments=n)
            dinv = jnp.where(deg > 0, jax.lax.rsqrt(deg), 0.0)
            norm = dinv[s] * dinv[d]
            msg = h[s] * norm[:, None]
            out = jax.ops.segment_sum(msg, d, num_segments=n)
            return out + b
        key = jax.random.key(seed)
        k0, k1, k2, k3, k4 = jax.random.split(key, 5)
        x = jax.random.normal(k0, (N, 16), jnp.float32)
        edge_index = jax.random.randint(k1, (2, E), 0, N, dtype=jnp.int64)
        W1, b1 = _init_linear(k2, 16, 48)
        W2, b2 = _init_linear(k3, 48, 32)
        Wfc, bfc = _init_linear(k4, 32, N_CHANNEL)
        return {'x': x, 'edge_index': edge_index, 'W1': W1, 'b1': b1, 'W2': W2, 'b2': b2, 'Wfc': Wfc, 'bfc': bfc}
    _L0_gnn_all = _L0_gnn_setup()
    _L0_gnn_in = {k: v for k, v in _L0_gnn_all.items() if k in ('W1', 'b1', 'W2', 'b2', 'Wfc', 'bfc')}
    del _L0_gnn_all

    def _L1_gnn_setup():
        import jax, jax.numpy as jnp
        import numpy as np
        LATENT = 16
        KDIM = 128
        EDIM = 6
        DEPTH = 4
        N_NODES = 50000
        N_EDGES = 25000

        def _kernel_net(edge_attr, kW1, kb1, kW2, kb2, kW3, kb3):
            h = jax.nn.gelu(edge_attr @ kW1 + kb1)
            h = jax.nn.gelu(h @ kW2 + kb2)
            return h @ kW3 + kb3
        key = jax.random.key(seed)
        ks = jax.random.split(key, 12)
        inp = {'nodes': jax.random.normal(ks[0], (N_NODES, LATENT), dtype=jnp.float32), 'edge_index': jax.random.randint(ks[1], (2, N_EDGES), 0, N_NODES, dtype=jnp.int64), 'edge_attr': jax.random.uniform(ks[2], (N_EDGES, EDIM), dtype=jnp.float32), 'kW1': jax.random.normal(ks[3], (EDIM, KDIM), dtype=jnp.float32) / np.sqrt(EDIM), 'kb1': jnp.zeros((KDIM,), dtype=jnp.float32), 'kW2': jax.random.normal(ks[4], (KDIM, KDIM), dtype=jnp.float32) / np.sqrt(KDIM), 'kb2': jnp.zeros((KDIM,), dtype=jnp.float32), 'kW3': jax.random.normal(ks[5], (KDIM, LATENT * LATENT), dtype=jnp.float32) / np.sqrt(KDIM), 'kb3': jnp.zeros((LATENT * LATENT,), dtype=jnp.float32), 'root_W': jax.random.normal(ks[6], (DEPTH, LATENT, LATENT), dtype=jnp.float32) / np.sqrt(LATENT), 'root_b': jnp.zeros((DEPTH, LATENT), dtype=jnp.float32)}
        return inp
    _L1_gnn_all = _L1_gnn_setup()
    _L1_gnn_in = {k: v for k, v in _L1_gnn_all.items() if k in ('kW1', 'kb1', 'kW2', 'kb2', 'kW3', 'kb3', 'root_W', 'root_b')}
    del _L1_gnn_all

    def _L2_gnn_setup():
        import jax, jax.numpy as jnp
        import numpy as np
        N_NODES = 3125
        N_EDGES = 100000
        NUM_REL = 8

        def _rgcn_layer(x, src, dst, edge_type, W, root, bias):
            out = x @ root + bias
            x_src = x[src]
            for r in range(W.shape[0]):
                mask = (edge_type == r).astype(x.dtype)
                s = jax.ops.segment_sum(x_src * mask[:, None], dst, num_segments=x.shape[0])
                cnt = jax.ops.segment_sum(mask, dst, num_segments=x.shape[0])
                agg = s / jnp.clip(cnt, 1.0)[:, None]
                out = out + agg @ W[r]
            return out
        key = jax.random.key(seed)
        ks = jax.random.split(key, 9)
        x = jax.random.normal(ks[0], (N_NODES, 16), dtype=jnp.float32)
        edge_index = jax.random.randint(ks[1], (2, N_EDGES), 0, N_NODES, dtype=jnp.int32)
        edge_type = jax.random.randint(ks[2], (N_EDGES,), 0, NUM_REL, dtype=jnp.int32)
        s1 = 1.0 / np.sqrt(16.0)
        s2 = 1.0 / np.sqrt(32.0)
        W1 = jax.random.normal(ks[3], (NUM_REL, 16, 32), dtype=jnp.float32) * s1
        root1 = jax.random.normal(ks[4], (16, 32), dtype=jnp.float32) * s1
        b1 = jnp.zeros((32,), dtype=jnp.float32)
        W2 = jax.random.normal(ks[5], (NUM_REL, 32, 16), dtype=jnp.float32) * s2
        root2 = jax.random.normal(ks[6], (32, 16), dtype=jnp.float32) * s2
        b2 = jnp.zeros((16,), dtype=jnp.float32)
        return {'x': x, 'edge_index': edge_index, 'edge_type': edge_type, 'W1': W1, 'root1': root1, 'b1': b1, 'W2': W2, 'root2': root2, 'b2': b2}
    _L2_gnn_all = _L2_gnn_setup()
    _L2_gnn_in = {k: v for k, v in _L2_gnn_all.items() if k in ('W1', 'root1', 'b1', 'W2', 'root2', 'b2')}
    del _L2_gnn_all

    def _L3_gnn_setup():
        import jax, jax.numpy as jnp
        import numpy as np
        N_NODES = 30000
        N_EDGES = 9375
        IN_FEATS = 16
        OUT_FEATS = 16
        EDGE_DIM = 16
        key = jax.random.key(seed)
        ks = jax.random.split(key, 8)
        feat = jax.random.normal(ks[0], (N_NODES, IN_FEATS), dtype=jnp.float32)
        efeat = jax.random.normal(ks[1], (N_EDGES, EDGE_DIM), dtype=jnp.float32)
        W_msg = jax.random.normal(ks[2], (EDGE_DIM, IN_FEATS * OUT_FEATS), dtype=jnp.float32) * 0.1
        b_msg = jnp.zeros((IN_FEATS * OUT_FEATS,), dtype=jnp.float32)
        W_attn = jax.random.normal(ks[3], (EDGE_DIM, IN_FEATS * OUT_FEATS), dtype=jnp.float32) * 0.1
        b_attn = jnp.zeros((IN_FEATS * OUT_FEATS,), dtype=jnp.float32)
        src = jax.random.randint(ks[4], (N_EDGES,), 0, N_NODES, dtype=jnp.int32)
        dst = jax.random.randint(ks[5], (N_EDGES,), 0, N_NODES, dtype=jnp.int32)
        return {'feat': feat, 'efeat': efeat, 'W_msg': W_msg, 'b_msg': b_msg, 'W_attn': W_attn, 'b_attn': b_attn, 'src': src, 'dst': dst}
    _L3_gnn_all = _L3_gnn_setup()
    _L3_gnn_in = {k: v for k, v in _L3_gnn_all.items() if k in ('W_msg', 'b_msg', 'W_attn', 'b_attn')}
    del _L3_gnn_all
    return {'x': x, 'src': src, 'dst': dst, 'edge_attr_16': edge_attr_16, 'edge_attr_6': edge_attr_6, 'edge_type_8': edge_type_8, 'L0_gnn_W1': _L0_gnn_in['W1'], 'L0_gnn_b1': _L0_gnn_in['b1'], 'L0_gnn_W2': _L0_gnn_in['W2'], 'L0_gnn_b2': _L0_gnn_in['b2'], 'L0_gnn_Wfc': _L0_gnn_in['Wfc'], 'L0_gnn_bfc': _L0_gnn_in['bfc'], 'L1_gnn_kW1': _L1_gnn_in['kW1'], 'L1_gnn_kb1': _L1_gnn_in['kb1'], 'L1_gnn_kW2': _L1_gnn_in['kW2'], 'L1_gnn_kb2': _L1_gnn_in['kb2'], 'L1_gnn_kW3': _L1_gnn_in['kW3'], 'L1_gnn_kb3': _L1_gnn_in['kb3'], 'L1_gnn_root_W': _L1_gnn_in['root_W'], 'L1_gnn_root_b': _L1_gnn_in['root_b'], 'L2_gnn_W1': _L2_gnn_in['W1'], 'L2_gnn_root1': _L2_gnn_in['root1'], 'L2_gnn_b1': _L2_gnn_in['b1'], 'L2_gnn_W2': _L2_gnn_in['W2'], 'L2_gnn_root2': _L2_gnn_in['root2'], 'L2_gnn_b2': _L2_gnn_in['b2'], 'L3_gnn_W_msg': _L3_gnn_in['W_msg'], 'L3_gnn_b_msg': _L3_gnn_in['b_msg'], 'L3_gnn_W_attn': _L3_gnn_in['W_attn'], 'L3_gnn_b_attn': _L3_gnn_in['b_attn']}

def reference(x, src, dst, edge_attr_16, edge_attr_6, edge_type_8, L0_gnn_W1, L0_gnn_b1, L0_gnn_W2, L0_gnn_b2, L0_gnn_Wfc, L0_gnn_bfc, L1_gnn_kW1, L1_gnn_kb1, L1_gnn_kW2, L1_gnn_kb2, L1_gnn_kW3, L1_gnn_kb3, L1_gnn_root_W, L1_gnn_root_b, L2_gnn_W1, L2_gnn_root1, L2_gnn_b1, L2_gnn_W2, L2_gnn_root2, L2_gnn_b2, L3_gnn_W_msg, L3_gnn_b_msg, L3_gnn_W_attn, L3_gnn_b_attn):
    import jax
    import jax.numpy as jnp

    def _L0_gnn_ref(x, edge_index, W1, b1, W2, b2, Wfc, bfc):
        import jax, jax.numpy as jnp
        import numpy as np
        N = 3125
        E = 100000
        N_CHANNEL = 16

        def _init_linear(key, fan_in, fan_out):
            bound = 1.0 / np.sqrt(fan_in)
            kw, kb = jax.random.split(key)
            W = jax.random.uniform(kw, (fan_in, fan_out), jnp.float32, -bound, bound)
            b = jax.random.uniform(kb, (fan_out,), jnp.float32, -bound, bound)
            return (W, b)

        def gcn_conv(x, W, b, src, dst, n):
            h = x @ W
            loop = jnp.arange(n, dtype=src.dtype)
            s = jnp.concatenate([src, loop])
            d = jnp.concatenate([dst, loop])
            deg = jax.ops.segment_sum(jnp.ones_like(s, dtype=h.dtype), d, num_segments=n)
            dinv = jnp.where(deg > 0, jax.lax.rsqrt(deg), 0.0)
            norm = dinv[s] * dinv[d]
            msg = h[s] * norm[:, None]
            out = jax.ops.segment_sum(msg, d, num_segments=n)
            return out + b
        src, dst = (edge_index[0], edge_index[1])
        h = jax.nn.relu(gcn_conv(x, W1, b1, src, dst, N))
        h = jax.nn.relu(gcn_conv(h, W2, b2, src, dst, N))
        return h @ Wfc + bfc

    def _L1_gnn_ref(nodes, edge_attr, kW1, kb1, kW2, kb2, kW3, kb3, root_W, root_b, edge_index):
        import jax, jax.numpy as jnp
        import numpy as np
        LATENT = 16
        KDIM = 128
        EDIM = 6
        DEPTH = 4
        N_NODES = 50000
        N_EDGES = 25000

        def _kernel_net(edge_attr, kW1, kb1, kW2, kb2, kW3, kb3):
            h = jax.nn.gelu(edge_attr @ kW1 + kb1)
            h = jax.nn.gelu(h @ kW2 + kb2)
            return h @ kW3 + kb3
        src, dst = (edge_index[0], edge_index[1])
        n = nodes.shape[0]
        w = _kernel_net(edge_attr, kW1, kb1, kW2, kb2, kW3, kb3).reshape(-1, LATENT, LATENT)
        deg = jax.ops.segment_sum(jnp.ones((src.shape[0],), nodes.dtype), dst, num_segments=n)
        inv_deg = jnp.where(deg > 0, 1.0 / jnp.maximum(deg, 1.0), 0.0)[:, None]
        for i in range(DEPTH):
            msg = jnp.einsum('ei,eio->eo', nodes[src], w)
            agg = jax.ops.segment_sum(msg, dst, num_segments=n)
            agg = agg * inv_deg
            nodes = jax.nn.gelu(agg + nodes @ root_W[i] + root_b[i])
        return nodes

    def _L2_gnn_ref(x, edge_index, edge_type, W1, root1, b1, W2, root2, b2):
        import jax, jax.numpy as jnp
        import numpy as np
        N_NODES = 3125
        N_EDGES = 100000
        NUM_REL = 8

        def _rgcn_layer(x, src, dst, edge_type, W, root, bias):
            out = x @ root + bias
            x_src = x[src]
            for r in range(W.shape[0]):
                mask = (edge_type == r).astype(x.dtype)
                s = jax.ops.segment_sum(x_src * mask[:, None], dst, num_segments=x.shape[0])
                cnt = jax.ops.segment_sum(mask, dst, num_segments=x.shape[0])
                agg = s / jnp.clip(cnt, 1.0)[:, None]
                out = out + agg @ W[r]
            return out
        src, dst = (edge_index[0], edge_index[1])
        h = _rgcn_layer(x, src, dst, edge_type, W1, root1, b1)
        h = jax.nn.relu(h)
        h = _rgcn_layer(h, src, dst, edge_type, W2, root2, b2)
        return h

    def _L3_gnn_ref(feat, efeat, W_msg, b_msg, W_attn, b_attn, src, dst):
        import jax, jax.numpy as jnp
        import numpy as np
        N_NODES = 30000
        N_EDGES = 9375
        IN_FEATS = 16
        OUT_FEATS = 16
        EDGE_DIM = 16
        N, in_f = feat.shape
        E = efeat.shape[0]
        w_m = (efeat @ W_msg + b_msg).reshape(E, in_f, -1)
        w_a = (efeat @ W_attn + b_attn).reshape(E, in_f, -1)
        h_src = feat[src][:, :, None]
        e1 = w_m * h_src
        e2 = w_a * h_src
        seg_max = jax.ops.segment_max(e2, dst, num_segments=N)
        ex = jnp.exp(e2 - seg_max[dst])
        denom = jax.ops.segment_sum(ex, dst, num_segments=N)
        attn = ex / denom[dst]
        ft = jax.ops.segment_sum(e1 * attn, dst, num_segments=N)
        return ft.sum(axis=1)
    edge_index = jnp.stack([src, dst])
    x = _layernorm(x + _L0_gnn_ref(x, edge_index, L0_gnn_W1, L0_gnn_b1, L0_gnn_W2, L0_gnn_b2, L0_gnn_Wfc, L0_gnn_bfc), axis=-1)
    x = _layernorm(x + _L1_gnn_ref(x, edge_attr_6, L1_gnn_kW1, L1_gnn_kb1, L1_gnn_kW2, L1_gnn_kb2, L1_gnn_kW3, L1_gnn_kb3, L1_gnn_root_W, L1_gnn_root_b, edge_index), axis=-1)
    x = _layernorm(x + _L2_gnn_ref(x, edge_index, edge_type_8, L2_gnn_W1, L2_gnn_root1, L2_gnn_b1, L2_gnn_W2, L2_gnn_root2, L2_gnn_b2), axis=-1)
    x = _layernorm(x + _L3_gnn_ref(x, edge_attr_16, L3_gnn_W_msg, L3_gnn_b_msg, L3_gnn_W_attn, L3_gnn_b_attn, src, dst), axis=-1)
    return x

_drawn_inputs = setup_inputs


def setup_inputs(seed=0):
    import zlib

    import numpy as np

    out = dict(_drawn_inputs(seed))
    spreads = {'L1_gnn_kb1': (0.0, 0.295),
     'L1_gnn_kb2': (0.0, 0.1),
     'L1_gnn_kb3': (0.0, 0.1),
     'L1_gnn_root_b': (0.0, 0.337),
     'L2_gnn_b1': (0.0, 0.268),
     'L2_gnn_b2': (0.0, 0.688),
     'L3_gnn_b_msg': (0.0, 0.1),
     'L3_gnn_b_attn': (0.0, 2.0)}
    factors = {'edge_attr_6': 15.442, 'L0_gnn_W1': 28.33, 'L0_gnn_b1': 29.984, 'x': 3.457}
    for name, (base, spread) in spreads.items():
        noise = np.random.default_rng([zlib.crc32(name.encode()), seed]).standard_normal(out[name].shape)
        drawn = base * np.exp(spread * noise) if base else spread * noise
        out[name] = jnp.asarray(drawn.astype(out[name].dtype))
    for name, factor in factors.items():
        out[name] = (out[name] * factor).astype(out[name].dtype)
    return out
```

```python
from contextlib import ExitStack

import concourse.bass as bass
from concourse import mybir

F32 = mybir.dt.float32
BF16 = mybir.dt.bfloat16
I32 = mybir.dt.int32
ALU = mybir.AluOpType
ACT = mybir.ActivationFunctionType
AX_X = mybir.AxisListType.X

P = 128
N, E, LAT = 3125, 103125, 16
NP, NT = 125, 25
COLS = -(-E // P)
CH = 26
NCH = COLS // CH
HALF = NCH // 2
PAIRS = CH // 2
REL = 8
KD = 128
DEPTH = 4
EPS = 1e-5
BIG = 3.0e38
SKIP = 4096
J3 = 13
N3 = COLS // J3
CC = 256
STAGES = [("gcn1", 16, "plain"), ("gcn2", 32, "plain")] + [(f"nnconv{i}", 16, "mlp") for i in range(DEPTH)] \
    + [("rgcn1", 32, "weighted"), ("rgcn2", 16, "weighted")]
assert NP * NT == N and NCH * CH == COLS and N3 * J3 == COLS and NCH % 2 == 1


def over_chunks(eng, body):
    body(0, 0)
    body(1, 1)
    with eng.Fori(1, HALF) as turn:
        body(turn * 2, 0)
        body(turn * 2 + 1, 1)
    body(NCH - 1, 0)


def over_chunks3(eng, body):
    body(0, 0)
    body(1, 1)
    with eng.Fori(1, N3 // 2 - 1) as turn:
        body(turn * 2, 0)
        body(turn * 2 + 1, 1)
    body(N3 - 2, 0)
    body(N3 - 1, 1)


def known(k):
    return isinstance(k, int)


def half(k):
    return k // 2


def build(nc, x, src, dst, ends, etype, eaT, efT, W1, b1, W2, b2, Wfc, bfc, kW1, kb1, kW2, kb2, kW3, kb3,
          rootW, rootb, RW1, Rroot1, Rb1, RW2, Rroot2, Rb2, Wm, bm, Wa, ba, out, upto=9):
    with ExitStack() as ctx:
        def sb(name, shape, dt=F32):
            return ctx.enter_context(nc.sbuf_tensor(name, shape, dt))

        def sem(name):
            return ctx.enter_context(nc.semaphore(name))

        def dram(name, shape, dt=F32):
            return nc.dram_tensor(name, shape, dt, kind="Internal").ap()

        table16 = dram("table16", [N, 16])
        table32 = dram("table32", [N, 32])
        rel32 = dram("rel32", [N * REL, 32])
        rel16 = dram("rel16", [N * REL, 16])
        sums16 = dram("sums16", [P * COLS, 16])
        sums32 = dram("sums32", [P * COLS, 32])
        dst_rows = dram("dst_rows", [P, COLS])
        end_index = dram("end_index", [P, COLS], I32)
        neg_flags = dram("neg_flags", [P, COLS])
        attn_table = dram("attn_table", [N, 3 * CC])
        rel_index = dram("rel_index", [P, COLS], I32)
        tables = [table16, table32] + [table16] * DEPTH + [rel32, rel16]
        indices = [src] * (2 + DEPTH) + [rel_index] * 2

        notstart = sb("notstart", [P, COLS])
        weight = sb("weight", [P, COLS])
        spans = sb("spans", [P, N])
        ident = sb("ident", [P, P])
        last_edge = sb("last_edge", [NP, NT], I32)
        has = sb("has", [NP, NT])
        deg = sb("deg", [NP, NT])
        dinv = sb("dinv", [NP, NT])
        inv_deg = sb("inv_deg", [NP, NT])
        X = sb("X", [NP, NT, 16])
        nodes = sb("nodes", [NP, NT, 16])
        pace = sb("pace", [1, 2])
        chain = sb("chain", [P, P])
        fix_index = sb("fix_index", [P, 1], I32)
        end_of = sb("end_of", [P, 2, J3], I32)

        W1s = sb("W1s", [16, 48]); W2s = sb("W2s", [48, 32]); Wfcs = sb("Wfcs", [32, 16])
        b1s = sb("b1s", [NP, 48]); b2s = sb("b2s", [NP, 32]); bfcs = sb("bfcs", [NP, 16])
        kW1s = sb("kW1s", [6, KD]); kW2s = sb("kW2s", [KD, KD]); kW3s = sb("kW3s", [KD, CC])
        kb1s = sb("kb1s", [KD, 1]); kb2s = sb("kb2s", [KD, 1])
        kb3s = sb("kb3s", [1, CC]); kb3p = sb("kb3p", [1, 3, CC], BF16); kb3r = sb("kb3r", [1, 2, CC])
        kb3w = sb("kb3w", [3, 2, CC], BF16)
        ones3 = sb("ones3", [3, P], BF16)
        rootWs = sb("rootWs", [16, DEPTH, 16]); rootbs = sb("rootbs", [NP, DEPTH, 16])
        RW1s = sb("RW1s", [16, REL, 32]); Rroot1s = sb("Rroot1s", [16, 32]); Rb1s = sb("Rb1s", [NP, 32])
        RW2s = sb("RW2s", [32, REL, 16]); Rroot2s = sb("Rroot2s", [32, 16]); Rb2s = sb("Rb2s", [NP, 16])

        index = sb("index", [P, 2, CH], I32)
        ARENA = 40700
        arena = sb("arena", [P, ARENA])
        at = [0]

        def carve(parts, *shape, dt=F32):
            n = 1
            for d in shape:
                n *= d
            v = arena[0:parts, at[0]:at[0] + n]
            at[0] += n
            assert at[0] <= ARENA, at[0]
            if dt != F32:
                v = v.bitcast(dt)
            if len(shape) == 2:
                v = v.rearrange("p (a b) -> p a b", a=shape[0])
            if len(shape) == 3:
                v = v.rearrange("p (a b c) -> p a b c", a=shape[0], b=shape[1])
            return v

        rows = [[carve(P, CH, 32) for _ in range(2)] for _ in range(1)][0]
        scan_in = carve(P, 32, CH + 1)
        scan_flag = carve(P, 32, CH + 1)
        scan_out = carve(P, 32, CH + 1)
        scanned_rows = [carve(P, CH, 32) for _ in range(2)]
        eaTs = [carve(6, CH * P) for _ in range(2)]
        h1s = [carve(KD, 2 * P) for _ in range(2)]
        h2s = [carve(KD, 2 * P) for _ in range(2)]
        prod = [carve(P, 2, CC) for _ in range(2)]
        agg = carve(NP, NT, 32)
        feat = carve(NP, NT, 48)
        tmp = carve(NP, NT, 48)
        featT = carve(48, N)
        stat = sb("stat", [NP, 4, NT]); stat3 = sb("stat3", [1, 1])
        ysb = carve(NP, NT, CC)
        at[0] = 0
        dsti = carve(P, COLS, dt=I32)
        dstf = carve(P, COLS)
        typei = carve(P, COLS, dt=I32)
        typef = carve(P, COLS)
        nextsame = carve(P, COLS)
        relf = [carve(P, COLS) for _ in range(REL)]
        relsum = [carve(P, COLS) for _ in range(REL)]
        back = carve(P, COLS)
        total = carve(P, COLS)
        isfirst = carve(P, COLS)
        islast = carve(P, COLS)
        idxf = carve(P, COLS)
        srci = carve(P, COLS, dt=I32)
        iota_n = carve(P, N + 1, dt=I32)
        node_row = carve(P, N + 1)
        edge_rows = [carve(NP, COLS) for _ in range(2)]
        hits = carve(NP, COLS); hits_n = carve(P, N + 1)
        small = carve(P, 64)
        firstrow_i = carve(P, P, dt=I32); lastrow_i = carve(P, P, dt=I32)
        firstrow = carve(P, P); lastrow = carve(P, P)
        iota_c = carve(P, P, dt=I32); colno = carve(P, P)
        intake = carve(P, P); intake2 = carve(P, P)
        nexti = carve(P, 1, dt=I32)
        part_i = carve(P, 1, dt=I32)
        want_i = carve(NP, NT + 1, dt=I32); want = carve(NP, NT + 1)
        rowno_f = carve(NP, NT + 1); rowno = carve(NP, NT + 1, dt=I32)
        lower = carve(NP, NT + 1)
        lastf = carve(P, 2, REL)
        inout = carve(P, 2, REL)
        nodeq = carve(NP, NT); nodeq2 = carve(NP, NT); nodeq3 = carve(NP, NT)
        endf = carve(P, COLS); endi = carve(P, COLS, dt=I32); negf = carve(P, COLS)
        prevlast_row = carve(P, P); wholerow = carve(P, P)
        at[0] = 0
        scores = [carve(P, 2, CC * (J3 + 1)) for _ in range(2)]
        decay = carve(P, CC * (J3 + 1))
        attn_neg = carve(P, CC * (J3 + 1))
        peak = carve(P, CC * (J3 + 1))
        AFTER_PEAK = at[0]
        end_rows = carve(P, J3, 3 * CC)
        xrows = [carve(P, J3 * 16) for _ in range(2)]
        efTs = [carve(17, J3 * P) for _ in range(2)]
        zeros = carve(NP, 3 * CC)
        neg_in = [carve(P, J3) for _ in range(2)]
        Wcat = carve(17, 2, CC)
        at[0] = 0
        lastT = carve(P, 3, 2 * P)
        chainT = carve(P, 2 * P); peakT = carve(P, 2 * P); decT = carve(P, 2 * P); riseT = carve(P, 2 * P)
        denT = carve(P, 2 * P); numT = carve(P, 2 * P)
        shiftT = carve(P, 3, 2 * (P + 1))
        cin = carve(P, 3, CC); own = carve(P, 3 * CC); both = carve(P, 3 * CC)
        ea_ = carve(P, CC); eb_ = carve(P, CC)
        assert at[0] <= 2 * CC * (J3 + 1)
        at[0] = AFTER_PEAK
        node_att = carve(NP, NT, 2 * CC)
        nohas = carve(NP, NT)
        at[0] = 2 * CC * (J3 + 1) * 2
        summed = carve(NP, NT, 16); summed2 = carve(NP, NT, 16)
        colfirst, collast, nextfirst, spanval, partno, ones1, spaneq, spanneg = (small[:, i:i + 1] for i in range(8))

        ps = ctx.enter_context(nc.psum_tensor("ps", [P, 8, 512], F32))

        loaded = sem("loaded")
        n_loads = [0]
        made = sem("made")
        table_written = sem("table_written")
        index_loaded = [sem(f"index_loaded{s}") for s in range(2)]
        gathered = [sem(f"gathered{s}") for s in range(2)]
        paced = sem("paced")
        rows_taken = sem("rows_taken")
        flags_made = sem("flags_made")
        scanned = sem("scanned")
        carried = sem("carried")
        rows_scanned = sem("rows_scanned")
        stored = [sem(f"stored{s}") for s in range(2)]
        agg_gathered = sem("agg_gathered")
        spans_summed = sem("spans_summed")
        feat_ready = sem("feat_ready")
        transposed = sem("transposed")
        featT_ready = sem("featT_ready")
        dense_done = sem("dense_done")
        y_ready = sem("y_ready")
        y_taken = sem("y_taken")
        table_ready = sem("table_ready")
        to_sqrt = sem("to_sqrt"); sqrt_done = sem("sqrt_done")
        to_gelu = sem("to_gelu"); gelu_done = sem("gelu_done")
        ea_loaded = [sem(f"ea_loaded{s}") for s in range(2)]
        h1_ready = sem("h1_ready"); h1_made = sem("h1_made")
        h2_ready = sem("h2_ready"); h2_made = sem("h2_made")
        w_ready = sem("w_ready"); prod_done = sem("prod_done"); reduced = sem("reduced")
        pre_dma = sem("pre_dma"); pre_gather = [sem("pre_gather0"), sem("pre_gather1")]
        nexti_cleared = sem("nexti_cleared"); kb3_split = sem("kb3_split"); dstf_made = sem("dstf_made")
        relidx_made = sem("relidx_made"); rowno_made = sem("rowno_made"); below_made = sem("below_made")
        ends_counted = sem("ends_counted")
        pre_pe = sem("pre_pe"); pre_pe2 = sem("pre_pe2"); pre_pool = sem("pre_pool")
        out_done = sem("out_done")
        L3_loaded = [sem(f"L3_loaded{s}") for s in range(2)]
        end_loaded = [sem(f"end_loaded{s}") for s in range(2)]
        zeroed = sem("zeroed"); zeros_made = sem("zeros_made"); Wcat_loaded = sem("Wcat_loaded")
        x_gathered = [sem(f"x_gathered{s}") for s in range(2)]
        scattered = sem("scattered")
        wa_ready = sem("wa_ready"); scored = sem("scored")
        neg_made = sem("neg_made"); peaked = sem("peaked"); carries = sem("carries")
        risen = sem("risen"); risen_exp = sem("risen_exp")
        decay_begun = sem("decay_begun"); decayed = sem("decayed"); decay_exp = sem("decay_exp")
        weighted_msg = sem("weighted_msg"); den_done = sem("den_done"); num_done = sem("num_done")
        rows_made = sem("rows_made")
        tail_pe = sem("tail_pe"); tail_dve = sem("tail_dve"); tail_act = sem("tail_act"); tail_dma = sem("tail_dma")
        tail_gather = sem("tail_gather"); tail_scatter = sem("tail_scatter"); tail_ready = sem("tail_ready")
        shift_made = sem("shift_made"); own_cleared = sem("own_cleared"); fixed = sem("fixed")
        endidx_made = sem("endidx_made"); negf_made = sem("negf_made")

        DENSE = [(16, [(W1s[:, :], 48, 2)]), (48, [(W2s[:, :], 32, 2)]), (32, [(Wfcs[:, :], 16, 2)])] \
            + [(16, [(rootWs[:, i, :], 16, 7)]) for i in range(DEPTH)] \
            + [(16, [(Rroot1s[:, :], 32, 4)]), (32, [(Rroot2s[:, :], 16, 4)])]
        REL_W = {7: (RW1s[:, :, :].rearrange("p r c -> p (r c)"), 256), 8: (RW2s[:, :, :].rearrange("p r c -> p (r c)"), 128)}
        GROUP = 4
        NG = -(-NT // GROUP)

        def dense_out(bank, width, t):
            per = 512 // width
            return ps[0:NP, bank + t // per, (t % per) * width:(t % per + 1) * width]

        def dense_all(bank, width):
            per = 512 // width
            for t0 in range(0, NT, per):
                n = min(per, NT - t0)
                yield t0, n, ps[0:NP, bank + t0 // per, 0:n * width].rearrange("p (t c) -> p t c", c=width)

        block = ctx.enter_context(nc.Block())

        def span_bank(width):
            return 6

        LOADS = [
            (dsti[:, :], dst), (typei[:, :], etype), (srci[:, :], src),
            (firstrow_i[:, :], ends[0:1, :].broadcast_to([P, P])),
            (lastrow_i[:, :], ends[1:2, :].broadcast_to([P, P])),
            (X[:, :, :], x.rearrange("(p t) c -> p t c", t=NT)),
            (W1s[:, :], W1), (W2s[:, :], W2), (Wfcs[:, :], Wfc),
            (kW1s[:, :], kW1), (kW2s[:, :], kW2), (kW3s[:, :], kW3),
            (kb1s[:, :], kb1.rearrange("(p a) -> p a", a=1)), (kb2s[:, :], kb2.rearrange("(p a) -> p a", a=1)),
            (kb3s[:, :], kb3.rearrange("(a n) -> a n", a=1)),
            (rootWs[:, :, :], rootW.rearrange("d i o -> i d o")),
            (RW1s[:, :, :], RW1.rearrange("r i o -> i r o")), (RW2s[:, :, :], RW2.rearrange("r i o -> i r o")),
            (Rroot1s[:, :], Rroot1), (Rroot2s[:, :], Rroot2),
            (b1s[:, :], b1.rearrange("(a n) -> a n", a=1).broadcast_to([NP, 48])),
            (b2s[:, :], b2.rearrange("(a n) -> a n", a=1).broadcast_to([NP, 32])),
            (bfcs[:, :], bfc.rearrange("(a n) -> a n", a=1).broadcast_to([NP, 16])),
            (Rb1s[:, :], Rb1.rearrange("(a n) -> a n", a=1).broadcast_to([NP, 32])),
            (Rb2s[:, :], Rb2.rearrange("(a n) -> a n", a=1).broadcast_to([NP, 16])),
            (rootbs[:, :, :].rearrange("p d o -> p (d o)"),
             rootb.rearrange("(a d) o -> a (d o)", a=1).broadcast_to([NP, DEPTH * 16])),
        ]
        TABLE_FROM = [None] * 8

        @block.sync
        def _(sp):
            for to, frm in LOADS:
                sp.dma_start(to, frm).then_inc(loaded, 16)
            sp.wait_ge(nexti_cleared, 1)
            sp.dma_start(nexti[0:P - 1, :], ends[0:1, 1:P].rearrange("a p -> p a")).then_inc(pre_dma, 16)
            sp.wait_ge(kb3_split, 1)
            for i in range(3):
                for j in range(2):
                    sp.dma_start(kb3w[i:i + 1, j, :], kb3p[0:1, i, :]).then_inc(pre_dma, 16)
            sp.wait_ge(dstf_made, 1)
            sp.dma_start(dst_rows, dstf[:, :]).then_inc(pre_dma, 16)
            sp.wait_ge(relidx_made, 1)
            sp.dma_start(rel_index, srci[:, :]).then_inc(pre_dma, 16)

            sp.wait_ge(endidx_made, 1)
            sp.dma_start(end_index, endi).then_inc(pre_dma, 16)
            sp.wait_ge(negf_made, 1)
            sp.dma_start(neg_flags, negf).then_inc(pre_dma, 16)

            for st, (name, C, kind) in enumerate(STAGES[:upto]):
                sums = sums16 if C == 16 else sums32
                sums_v = sums.rearrange("(p k u) c -> p k (u c)", k=NCH, u=CH)
                idx_v = indices[st].rearrange("p (k u) -> p k u", u=CH)
                ea_v = eaT.rearrange("c (k n) -> c k n", k=NCH)
                sp.wait_ge(table_ready, st + 1)
                if kind == "weighted":
                    w = 256 if C == 32 else 128
                    sp.wait_ge(y_taken, NT * (st - 5))
                    sp.dma_start(tables[st].rearrange("(p t r) c -> p (t r c)", t=NT, r=REL),
                                 ysb[:, :, 0:w].rearrange("p t c -> p t c")).then_inc(table_written, 16)
                elif C == 32:
                    sp.dma_start(tables[st].rearrange("(p t) c -> p t c", t=NT), feat[:, :, 0:32]).then_inc(table_written, 16)
                else:
                    sp.dma_start(tables[st].rearrange("(p t) c -> p t c", t=NT),
                                 (nodes if st else feat)[:, :, 0:16]).then_inc(table_written, 16)
                ib = [16 * (HALF + 1) * st, 16 * HALF * st]
                gb = [16 * CH * (HALF + 1) * st, 16 * CH * HALF * st]

                def store(k, s):
                    sp.wait_ge(rows_scanned, NCH * st + k + 1)
                    sp.dma_start(sums_v[:, k, :], scanned_rows[s][:, 0:CH * C // 32, :].rearrange("p a b -> p (a b)"))\
                        .then_inc(stored[s], 16)

                def body(k, s):
                    if not isinstance(k, int) or k >= 2:
                        sp.wait_ge(gathered[s], half(k) * (16 * CH) + gb[s])
                    elif st:
                        sp.wait_ge(gathered[s], gb[s])
                    sp.dma_start(index[:, s, :], idx_v[:, k, :]).then_inc(index_loaded[s], 16)
                    if kind == "mlp":
                        d = st - 2
                        if not isinstance(k, int) or k >= 2:
                            sp.wait_ge(h1_ready, k * PAIRS + (NCH * PAIRS * d - PAIRS))
                        elif d:
                            sp.wait_ge(h1_ready, NCH * PAIRS * d)
                        sp.dma_start(eaTs[s], ea_v[:, k, :]).then_inc(ea_loaded[s], 16)
                    if not isinstance(k, int) or k >= 2:
                        store(k - 2, s)

                if st:
                    sp.wait_ge(agg_gathered, 16 * NT * st)
                over_chunks(sp, body)
                store(NCH - 2, 1)
                store(NCH - 1, 0)

            sp.wait_ge(table_ready, 9)
            sp.dma_start(table16.rearrange("(p t) c -> p t c", t=NT), X[:, :, :]).then_inc(table_written, 16)
            for half_, (w, b) in enumerate(((Wa, ba), (Wm, bm))):
                sp.dma_start(Wcat[0:16, half_, :], w).then_inc(Wcat_loaded, 16)
                sp.dma_start(Wcat[16:17, half_, :], b.rearrange("(a n) -> a n", a=1)).then_inc(Wcat_loaded, 16)
            sp.wait_ge(zeros_made, 1)
            for t in range(NT):
                sp.dma_start(attn_table[t * NP:(t + 1) * NP, :], zeros).then_inc(zeroed, 16)
            src3 = src.rearrange("p (k u) -> p k u", u=J3)
            end3 = end_index.rearrange("p (k u) -> p k u", u=J3)
            neg3 = neg_flags.rearrange("p (k u) -> p k u", u=J3)
            ef3 = efT.rearrange("c (k n) -> c k n", k=N3)

            def load_end(k, s):
                if not known(k) or k >= 2:
                    sp.wait_ge(scattered, k * (16 * J3) - 16 * J3)
                sp.dma_start(end_of[:, s, :], end3[:, k, :]).then_inc(end_loaded[s], 16)

            def load3(k, s):
                before = not known(k) or k >= 2
                if before:
                    sp.wait_ge(x_gathered[s], half(k) * (16 * J3))
                sp.dma_start(index[:, s, 0:J3], src3[:, k, :]).then_inc(L3_loaded[s], 16)
                if before:
                    sp.wait_ge(neg_made, k - 1)
                sp.dma_start(neg_in[s], neg3[:, k, :]).then_inc(L3_loaded[s], 16)
                if before:
                    sp.wait_ge(wa_ready, k * J3 - J3)
                sp.dma_start(efTs[s], ef3[:, k, :]).then_inc(L3_loaded[s], 16)
                if not known(k) or k >= 1:
                    load_end(k - 1, 1 - s)

            over_chunks3(sp, load3)
            load_end(N3 - 1, 1)
            sp.wait_ge(tail_scatter, 16)
            sp.dma_start(node_att, attn_table.rearrange("(p t) c -> p t c", t=NT)[:, :, CC:3 * CC]).then_inc(tail_dma, 16)
            sp.wait_ge(out_done, 1)
            sp.dma_start(out.rearrange("(p t) c -> p t c", t=NT), X[:, :, :]).then_inc(tail_dma, 16)
            sp.wait_ge(tail_dma, 32)

        @block.gpsimd
        def _(pool):
            nc.gpsimd.iota(iota_n, [[1, N + 1]], base=0, channel_multiplier=0).then_inc(pre_pool, 1)
            nc.gpsimd.iota(part_i, [[0, 1]], base=0, channel_multiplier=1).then_inc(pre_pool, 1)
            nc.gpsimd.iota(want_i, [[1, NT + 1]], base=0, channel_multiplier=NT).then_inc(pre_pool, 1)
            nc.gpsimd.memset(ident[:, :], 0.0).then_inc(pre_pool, 1)
            pool.wait_ge(pre_pool, 4)
            nc.gpsimd.affine_select(out=ident[:, :], in_=ident[:, :], compare_op=ALU.not_equal, fill=1.0, base=0,
                                    pattern=[[-1, P]], channel_multiplier=1).then_inc(pre_pool, 1)
            pool.wait_ge(rowno_made, 1)
            pool.wait_ge(pre_dma, 16 * 9)
            for t in range(NT + 1):
                if t >= 2:
                    pool.wait_ge(pre_pe2, t - 1)
                nc.gpsimd.indirect_dma_start(edge_rows[t % 2][:, :], None, dst_rows,
                                             bass.IndirectOffsetOnAxis(rowno[:, t:t + 1], 0)).then_inc(pre_gather[t % 2], 16)

            for st, (name, C, kind) in enumerate(STAGES[:upto]):
                ib = [16 * (HALF + 1) * st, 16 * HALF * st]
                pool.wait_ge(table_written, 16 * (st + 1))

                def body(k, s):
                    pool.wait_ge(index_loaded[s], half(k) * 16 + (ib[s] + 16))
                    if kind == "mlp":
                        if not isinstance(k, int) or k >= 2:
                            pool.wait_ge(prod_done, k * PAIRS + (NCH * PAIRS * (st - 2) - PAIRS))
                    elif not isinstance(k, int) or k >= 2:
                        taken = st if st < 2 else st - DEPTH
                        pool.wait_ge(rows_taken, k + (NCH * taken - 1))
                    if not isinstance(k, int):
                        pool.wait_ge(paced, k + (1 + (NCH - 3) * st - 2))
                        nc.gpsimd.tensor_tensor(pace[0:1, 0:1], pace[0:1, 1:2], pace[0:1, 1:2], ALU.add).then_inc(paced, 1)
                    for u in range(CH):
                        r = rows[s].rearrange("p a b -> p (a b)")
                        nc.gpsimd.indirect_dma_start(r[:, u * C:(u + 1) * C], None, tables[st],
                                                     bass.IndirectOffsetOnAxis(index[:, s, u:u + 1], 0))\
                            .then_inc(gathered[s], 16)

                over_chunks(pool, body)
                pool.wait_ge(stored[0], 16 * (HALF + 1) * (st + 1))
                pool.wait_ge(stored[1], 16 * HALF * (st + 1))
                aggf = agg.rearrange("p a b -> p (a b)")
                for t in range(NT):
                    nc.gpsimd.indirect_dma_start(aggf[:, t * C:(t + 1) * C], None, sums16 if C == 16 else sums32,
                                                 bass.IndirectOffsetOnAxis(last_edge[:, t:t + 1], 0)).then_inc(agg_gathered, 16)

            pool.wait_ge(table_written, 16 * 9)
            paced0 = 1 + (NCH - 3) * len(STAGES)

            def gather3(k, s):
                for u in range(J3):
                    nc.gpsimd.indirect_dma_start(xrows[s][:, u * 16:(u + 1) * 16], None, table16,
                                                 bass.IndirectOffsetOnAxis(index[:, s, u:u + 1], 0)).then_inc(x_gathered[s], 16)

            def scatter3(s):
                for u in range(J3):
                    nc.gpsimd.indirect_dma_start(attn_table, bass.IndirectOffsetOnAxis(end_of[:, s, u:u + 1], 0),
                                                 end_rows[:, u, :], None, bounds_check=N - 1, oob_is_err=False)\
                        .then_inc(scattered, 16)

            for k in range(2):
                pool.wait_ge(L3_loaded[k], 48)
                gather3(k, k)
            pool.wait_ge(zeroed, 16 * NT)

            def body3(k, s):
                pool.wait_ge(peaked, k + 1)
                if not known(k) or k >= 1:
                    pool.wait_ge(num_done, k)
                d3, n3, p3 = (a.rearrange("p (c u) -> p c u", u=J3 + 1) for a in (decay, attn_neg, peak))
                nc.gpsimd.tensor_tensor(d3[:, :, 1:J3 + 1], p3[:, :, 0:J3], n3[:, :, 1:J3 + 1], ALU.add).then_inc(decay_begun, 1)
                if not known(k) or k >= 1:
                    pool.wait_ge(end_loaded[1 - s], half(k + 1) * 16)
                    pool.wait_ge(rows_made, k * 3)
                if not known(k) or k + 2 < N3:
                    pool.wait_ge(scored, k * J3 + J3)
                    pool.wait_ge(L3_loaded[s], half(k) * 48 + 96)
                if not known(k):
                    pool.wait_ge(paced, k + (paced0 - 2))
                    nc.gpsimd.tensor_tensor(pace[0:1, 0:1], pace[0:1, 1:2], pace[0:1, 1:2], ALU.add).then_inc(paced, 1)
                if not known(k) or k >= 1:
                    scatter3(1 - s)
                if not known(k) or k + 2 < N3:
                    gather3(k + 2, s)

            over_chunks3(pool, body3)
            pool.wait_ge(end_loaded[1], 16 * (N3 // 2))
            pool.wait_ge(rows_made, 3 * N3)
            scatter3(1)
            pool.wait_ge(scattered, 16 * J3 * N3)
            pool.wait_ge(own_cleared, 1)
            nc.gpsimd.indirect_dma_start(own, None, attn_table, bass.IndirectOffsetOnAxis(fix_index[:, :], 0),
                                         bounds_check=N - 1, oob_is_err=False).then_inc(tail_gather, 16)
            pool.wait_ge(fixed, 1)
            nc.gpsimd.indirect_dma_start(attn_table, bass.IndirectOffsetOnAxis(fix_index[:, :], 0), both, None,
                                         bounds_check=N - 1, oob_is_err=False).then_inc(tail_scatter, 16)

        @block.scalar
        def _(act):
            def dense_copies(d):
                cin = DENSE[d][0]
                for g in range(NG):
                    n = min(GROUP, NT - g * GROUP) * NP
                    act.wait_ge(transposed, NG * d + g + 1)
                    if d and g == 0:
                        act.wait_ge(dense_done, d)
                    nc.scalar.activation(featT[0:cin, g * GROUP * NP:g * GROUP * NP + n], ps[0:cin, g % 2, 0:n],
                                         ACT.Copy).then_inc(featT_ready, 1)

            def sqrt(n):
                act.wait_ge(to_sqrt, n)
                nc.scalar.activation(stat[:, 3, :], stat[:, 2, :], ACT.Sqrt).then_inc(sqrt_done, 1)

            sqrt(1)
            dense_copies(0)
            dense_copies(1)
            dense_copies(2)
            sqrt(2)
            for d in range(DEPTH):
                if upto <= 2 + d:
                    return
                dense_copies(3 + d)
                q0 = NCH * PAIRS * d

                def make_h1(q, b):
                    act.wait_ge(h1_ready, q + (q0 + 1))
                    nc.scalar.activation(h1s[b], ps[:, 2 + b, 0:2 * P], ACT.Gelu_apprx_tanh, bias=kb1s[:, 0:1]).then_inc(h1_made, 1)

                def make_h2(q, b):
                    act.wait_ge(h2_ready, q + (q0 + 1))
                    nc.scalar.activation(h2s[b], ps[:, 4 + b, 0:2 * P], ACT.Gelu_apprx_tanh, bias=kb2s[:, 0:1]).then_inc(h2_made, 1)

                def body(k, s):
                    for i in range(PAIRS):
                        b = (PAIRS * s + i) % 2
                        make_h1(k * PAIRS + i, b)
                        if not (isinstance(k, int) and k == 0 and i == 0):
                            make_h2(k * PAIRS + (i - 1), 1 - b)

                over_chunks(act, body)
                make_h2(NCH * PAIRS - 1, (NCH * PAIRS - 1) % 2)
                act.wait_ge(to_gelu, d + 1)
                nc.scalar.activation(nodes[:, :, :], tmp[:, :, 0:16], ACT.Gelu_apprx_tanh).then_inc(gelu_done, 1)
            sqrt(3)
            for n, d in enumerate((7, 8)):
                if upto <= 6 + n:
                    return
                dense_copies(d)
                w = REL_W[d][1]
                for t in range(NT):
                    act.wait_ge(y_ready, NT * n + t + 1)
                    nc.scalar.activation(ysb[:, t, 0:w], ps[0:NP, 2 + t % 2, 0:w], ACT.Copy).then_inc(y_taken, 1)
            sqrt(4)
            n3 = attn_neg.rearrange("p (c u) -> p c u", u=J3 + 1)
            p3 = peak.rearrange("p (c u) -> p c u", u=J3 + 1)
            d3 = decay.rearrange("p (c u) -> p c u", u=J3 + 1)

            def make_neg(k, s):
                act.wait_ge(L3_loaded[s], half(k) * 48 + 48)
                nc.scalar.activation(n3[:, :, 1:J3 + 1], neg_in[s].unsqueeze(1).broadcast_to([P, CC, J3]), ACT.Copy)\
                    .then_inc(neg_made, 1)

            def body3(k, s):
                e3 = scores[s][:, 0, :].rearrange("p (c u) -> p c u", u=J3 + 1)
                t3 = scores[s][:, 1, :].rearrange("p (c u) -> p c u", u=J3 + 1)
                act.wait_ge(risen, k + 1)
                nc.scalar.activation(e3[:, :, 1:J3 + 1], e3[:, :, 1:J3 + 1], ACT.Exp).then_inc(risen_exp, 1)
                if not known(k) or k + 1 < N3:
                    act.wait_ge(decay_begun, k + 1)
                    make_neg(k + 1, 1 - s)
                act.wait_ge(decayed, k + 1)
                nc.scalar.activation(d3[:, :, 1:J3 + 1], d3[:, :, 1:J3 + 1], ACT.Exp).then_inc(decay_exp, 1)
                if not known(k) or k >= 1:
                    act.wait_ge(scattered, k * (16 * J3))
                for n, (a, ready, count) in enumerate(((p3, None, 0), (e3, den_done, 1), (t3, num_done, 1))):
                    if ready is not None:
                        act.wait_ge(ready, k + 1)
                    nc.scalar.activation(end_rows[:, :, n * CC:(n + 1) * CC],
                                         a[:, :, 1:J3 + 1].rearrange("p c u -> p u c"), ACT.Copy).then_inc(rows_made, 1)

            act.wait_ge(zeros_made, 1)
            make_neg(0, 0)
            over_chunks3(act, body3)
            act.wait_ge(tail_dve, 1)
            nc.scalar.activation(riseT, riseT, ACT.Exp).then_inc(tail_act, 1)
            act.wait_ge(tail_dve, 2)
            nc.scalar.activation(decT, decT, ACT.Exp).then_inc(tail_act, 1)
            act.wait_ge(tail_dve, 3)
            nc.scalar.activation(ea_, ea_, ACT.Exp).then_inc(tail_act, 1)
            act.wait_ge(tail_dve, 4)
            nc.scalar.activation(eb_, eb_, ACT.Exp).then_inc(tail_act, 1)
            sqrt(5)

        @block.tensor
        def _(pe):
            pe.wait_ge(loaded, 16 * len(LOADS))
            pe.wait_ge(pre_pool, 5)
            pe.wait_ge(below_made, 1)
            for t in range(NT + 1):
                m = nc.tensor.matmul(ps[0:NP, 6, t:t + 1], hits_n[:, t:t + NT * (NP - 1) + 1:NT], ones1, start=True, stop=True)
            m.then_inc(pre_pe, 1)
            pe.wait_ge(ends_counted, 1)
            nc.tensor.matmul(ps[:, 7, 0:REL], intake, lastf[:, 0, :], start=True, stop=True)
            nc.tensor.matmul(ps[:, 7, REL:2 * REL], intake2, lastf[:, 1, :], start=True, stop=True).then_inc(pre_pe, 1)

            def dense(d):
                cin, products = DENSE[d]
                src_t = feat if d < 3 or d == 8 else (nodes if d < 7 else X)
                pe.wait_ge(feat_ready, d + 1)
                for g in range(NG):
                    if NG * d + g >= 2:
                        pe.wait_ge(featT_ready, NG * d + g - 1)
                    for j in range(min(GROUP, NT - g * GROUP)):
                        m = nc.tensor.transpose(ps[0:cin, g % 2, j * NP:(j + 1) * NP],
                                                src_t[:, g * GROUP + j, 0:cin], ident[0:NP, 0:NP])
                    m.then_inc(transposed, 1)
                pe.wait_ge(featT_ready, NG * (d + 1))
                for W, width, bank in products:
                    for t in range(NT):
                        m = nc.tensor.matmul(dense_out(bank, width, t), featT[0:cin, t * NP:(t + 1) * NP], W,
                                             start=True, stop=True)
                m.then_inc(dense_done, 1)
                if d in REL_W:
                    n = d - 7
                    W, width = REL_W[d]
                    for t in range(NT):
                        if NT * n + t >= 2:
                            pe.wait_ge(y_taken, NT * n + t - 1)
                        nc.tensor.matmul(ps[0:NP, 2 + t % 2, 0:width], featT[0:cin, t * NP:(t + 1) * NP], W,
                                         start=True, stop=True).then_inc(y_ready, 1)

            def span_sums(st, C):
                pe.wait_ge(rows_scanned, NCH * (st + 1))
                last = scanned_rows[0].rearrange("p a b -> p (a b)")[:, (CH - 1) * C:CH * C]
                for t in range(NT):
                    m = nc.tensor.matmul(dense_out(span_bank(C), C, t), spans[:, t:t + NT * (NP - 1) + 1:NT], last,
                                         start=True, stop=True)
                m.then_inc(spans_summed, 1)

            for st, (name, C, kind) in enumerate(STAGES[:upto]):
                if kind == "mlp":
                    d = st - 2
                    dense(3 + d)
                    q0 = NCH * PAIRS * d

                    def first(q, b, s, i):
                        if not isinstance(q, int) or q0 + q >= 2:
                            pe.wait_ge(h1_made, q + (q0 - 1))
                        nc.tensor.matmul(ps[:, 2 + b, 0:2 * P], kW1s[:, :], eaTs[s][:, i * 2 * P:(i + 1) * 2 * P],
                                         start=True, stop=True).then_inc(h1_ready, 1)

                    def second(q, b):
                        pe.wait_ge(h1_made, q + (q0 + 1))
                        if not isinstance(q, int) or q0 + q >= 2:
                            pe.wait_ge(h2_made, q + (q0 - 1))
                        nc.tensor.matmul(ps[:, 4 + b, 0:2 * P], kW2s[:, :], h1s[b], start=True, stop=True).then_inc(h2_ready, 1)

                    def third(q, b):
                        pe.wait_ge(h2_made, q + (q0 + 1))
                        if not isinstance(q, int) or q0 + q >= 2:
                            pe.wait_ge(prod_done, q + (q0 - 1))
                        nc.tensor.matmul(ps[:, b, :], ones3[:, :], kb3w[:, :, :].rearrange("p a b -> p (a b)"),
                                         start=True, stop=False, skip_group_check=True)
                        for j in range(2):
                            m = nc.tensor.matmul(ps[:, b, j * CC:(j + 1) * CC], h2s[b][:, j * P:(j + 1) * P], kW3s[:, :],
                                                 start=False, stop=(j == 1), skip_group_check=True)
                        m.then_inc(w_ready, 1)

                    def body(k, s):
                        lb = [16 * (HALF + 1) * d, 16 * HALF * d]
                        pe.wait_ge(ea_loaded[s], half(k) * 16 + (lb[s] + 16))
                        for i in range(PAIRS):
                            b = (PAIRS * s + i) % 2
                            q = k * PAIRS + i
                            first(q, b, s, i)
                            if not (isinstance(k, int) and q < 1):
                                second(k * PAIRS + (i - 1), 1 - b)
                            if not (isinstance(k, int) and q < 2):
                                third(k * PAIRS + (i - 2), b)

                    over_chunks(pe, body)
                    Q = NCH * PAIRS
                    second(Q - 1, (Q - 1) % 2)
                    third(Q - 2, (Q - 2) % 2)
                    third(Q - 1, (Q - 1) % 2)
                if kind == "weighted":
                    dense(st + 1)
                span_sums(st, C)
                if st == 0:
                    dense(0)
                    dense(1)
                if st == 1:
                    dense(2)

            pe.wait_ge(Wcat_loaded, 64)
            pe.wait_ge(tail_ready, 1)
            RING = 7

            def body3(k, s):
                pe.wait_ge(L3_loaded[s], half(k) * 48 + 48)
                for u in range(J3):
                    back_ = RING if u >= RING else (RING - 1 if u < J3 - RING else J3)
                    if not known(k) or k * J3 + u - back_ >= 0:
                        pe.wait_ge(scored, k * J3 + (u - back_ + 1))
                    nc.tensor.matmul(ps[:, u % RING, :], efTs[s][:, u * P:(u + 1) * P],
                                     Wcat.rearrange("p a b -> p (a b)"), start=True, stop=True).then_inc(wa_ready, 1)

            over_chunks3(pe, body3)
            pe.wait_ge(num_done, N3)
            pe.wait_ge(scored, N3 * J3)
            u = J3 + 1
            pe.wait_ge(peaked, N3)
            for h in range(2):
                pk = peak.rearrange("p (c u) -> p c u", u=u)[:, h * P:(h + 1) * P, J3]
                nc.tensor.transpose(ps[:, 0, h * P:(h + 1) * P], pk, ident[:, :])
                for q in range(2):
                    st_ = scores[1][:, q, :].rearrange("p (c u) -> p c u", u=u)[:, h * P:(h + 1) * P, J3]
                    m = nc.tensor.transpose(ps[:, 1 + q, h * P:(h + 1) * P], st_, ident[:, :])
            m.then_inc(tail_pe, 1)
            pe.wait_ge(shift_made, 1)
            for q in range(3):
                for h in range(2):
                    m = nc.tensor.transpose(ps[:, 3 + q, h * P:(h + 1) * P], shiftT[:, q, h * (P + 1):h * (P + 1) + P], ident[:, :])
            m.then_inc(tail_pe, 1)

        @block.vector
        def _(dve):
            v = nc.vector
            n_made = [0]

            def step(ins):
                ins.then_inc(made, 1)
                n_made[0] += 1
                dve.wait_ge(made, n_made[0])

            v.memset(nexti, -1).then_inc(nexti_cleared, 1)
            v.memset(pace[:, :], 0.0).then_inc(paced, 1)
            step(v.memset(ones3[:, :], 1.0))
            step(v.memset(ones1, 1.0))
            dve.wait_ge(loaded, 16 * len(LOADS))
            step(v.tensor_copy(kb3p[:, 0, :], kb3s[:, :]))
            step(v.tensor_tensor(kb3r[:, 0, :], kb3s[:, :], kb3p[:, 0, :], ALU.subtract))
            step(v.tensor_copy(kb3p[:, 1, :], kb3r[:, 0, :]))
            step(v.tensor_tensor(kb3r[:, 1, :], kb3r[:, 0, :], kb3p[:, 1, :], ALU.subtract))
            v.tensor_copy(kb3p[:, 2, :], kb3r[:, 1, :]).then_inc(kb3_split, 1)
            v.tensor_copy(dstf, dsti).then_inc(dstf_made, 1)
            dve.wait_ge(dstf_made, 1)
            step(v.tensor_copy(colfirst, dstf[:, 0:1]))
            step(v.tensor_copy(collast, dstf[:, COLS - 1:COLS]))
            dve.wait_ge(pre_pool, 5)
            step(v.tensor_copy(node_row, iota_n))
            v.tensor_scalar(hits_n, node_row, collast, None, ALU.is_gt).then_inc(below_made, 1)
            step(v.tensor_copy(typef, typei))
            step(v.tensor_copy(total, srci))
            step(v.scalar_tensor_tensor(out=idxf, in0=total, scalar=float(REL), in1=typef, op0=ALU.mult, op1=ALU.add))
            v.tensor_copy(srci, idxf).then_inc(relidx_made, 1)
            step(v.tensor_copy(want, want_i))
            dve.wait_ge(pre_pe, 1)
            step(v.tensor_copy(rowno_f, ps[0:NP, 6, 0:NT + 1]))
            v.tensor_copy(rowno, rowno_f).then_inc(rowno_made, 1)
            for t in range(NT + 1):
                dve.wait_ge(pre_gather[t % 2], 16 * (t // 2 + 1))
                if t:
                    dve.wait_ge(pre_pe2, t)
                v.tensor_scalar(hits, edge_rows[t % 2], want[:, t:t + 1], 0.0, ALU.is_lt, ALU.add,
                                accum_out=lower[:, t:t + 1]).then_inc(pre_pe2, 1)
            dve.wait_ge(pre_pe2, NT + 1)
            step(v.scalar_tensor_tensor(out=lower, in0=rowno_f, scalar=float(COLS), in1=lower, op0=ALU.mult, op1=ALU.add))
            step(v.tensor_tensor(deg[:, :], lower[:, 1:NT + 1], lower[:, 0:NT], ALU.subtract))
            step(v.tensor_scalar(nodeq, lower[:, 1:NT + 1], -1.0, 0.0, ALU.add, ALU.max))
            step(v.tensor_copy(last_edge[:, :], nodeq))
            step(v.tensor_scalar(has[:, :], deg[:, :], 0.0, None, ALU.is_gt))
            step(v.tensor_scalar(nodeq2, deg[:, :], 1.0, None, ALU.max))
            step(v.reciprocal(nodeq3, nodeq2))
            step(v.tensor_tensor(inv_deg[:, :], nodeq3, has[:, :], ALU.mult))
            step(v.memset(notstart[:, 0:1], 0.0))
            step(v.tensor_tensor(notstart[:, 1:COLS], dstf[:, 1:COLS], dstf[:, 0:COLS - 1], ALU.is_equal))
            step(v.memset(nextsame[:, COLS - 1:COLS], 0.0))
            step(v.tensor_tensor(nextsame[:, 0:COLS - 1], dstf[:, 1:COLS], dstf[:, 0:COLS - 1], ALU.is_equal))
            dve.wait_ge(pre_dma, 16 * 9)
            step(v.tensor_copy(nextfirst, nexti))
            step(v.tensor_tensor(spaneq, collast, nextfirst, ALU.is_equal))
            step(v.scalar_tensor_tensor(out=spanval, in0=collast, scalar=1.0, in1=spaneq, op0=ALU.add, op1=ALU.mult))
            step(v.tensor_scalar(spanneg, spanval, -1.0, None, ALU.add))
            step(v.tensor_scalar(spans[:, :], node_row[:, 0:N], spanneg, None, ALU.is_equal))
            step(v.tensor_copy(endf, nextsame))
            step(v.tensor_copy(endf[:, COLS - 1:COLS], spaneq))
            step(v.scalar_tensor_tensor(out=endf, in0=endf, scalar=float(SKIP), in1=dstf, op0=ALU.mult, op1=ALU.add))
            v.tensor_copy(endi, endf).then_inc(endidx_made, 1)
            v.tensor_scalar(negf, notstart[:, :], -1.0, BIG, ALU.add, ALU.mult).then_inc(negf_made, 1)
            step(v.tensor_copy(partno, part_i))
            step(v.tensor_copy(firstrow, firstrow_i))
            step(v.tensor_copy(lastrow, lastrow_i))
            step(v.tensor_tensor(wholerow, firstrow, lastrow, ALU.is_equal))
            step(v.memset(prevlast_row[:, 0:1], 0.0))
            step(v.tensor_tensor(prevlast_row[:, 1:P], lastrow[:, 0:P - 1], firstrow[:, 1:P], ALU.is_equal))
            step(v.tensor_tensor(wholerow, wholerow, prevlast_row, ALU.mult))
            step(v.tensor_scalar(chain[:, :], wholerow, -1.0, BIG, ALU.add, ALU.mult))
            step(v.tensor_scalar(wholerow, node_row[:, 0:P], partno, None, ALU.is_equal))
            step(v.tensor_tensor(wholerow, wholerow, prevlast_row, ALU.mult))
            step(v.tensor_reduce(small[:, 8:9], wholerow, AX_X, ALU.add))
            step(v.tensor_tensor(small[:, 9:10], colfirst, collast, ALU.is_equal))
            step(v.tensor_tensor(small[:, 10:11], small[:, 9:10], spaneq, ALU.mult))
            step(v.tensor_scalar(small[:, 11:12], small[:, 10:11], -1.0, 1.0, ALU.mult, ALU.add))
            step(v.tensor_tensor(small[:, 12:13], small[:, 11:12], small[:, 8:9], ALU.mult))
            step(v.tensor_scalar(small[:, 13:14], small[:, 12:13], -float(SKIP), float(SKIP), ALU.mult, ALU.add))
            step(v.tensor_tensor(small[:, 14:15], small[:, 13:14], colfirst, ALU.add))
            step(v.tensor_copy(fix_index[:, :], small[:, 14:15]))
            step(v.tensor_scalar(colno, node_row[:, 0:P], partno, None, ALU.is_gt))
            step(v.tensor_scalar(firstrow, firstrow, collast, None, ALU.is_equal))
            step(v.tensor_tensor(intake, firstrow, colno, ALU.mult))
            step(v.tensor_scalar(colno, node_row[:, 0:P], partno, None, ALU.is_lt))
            step(v.tensor_scalar(lastrow, lastrow, colfirst, None, ALU.is_equal))
            step(v.tensor_tensor(intake2, lastrow, colno, ALU.mult))
            step(v.tensor_scalar(isfirst, dstf, colfirst, None, ALU.is_equal))
            step(v.tensor_scalar(islast, dstf, collast, None, ALU.is_equal))
            for r in range(REL):
                step(v.tensor_scalar(relf[r], typef, float(r), None, ALU.is_equal))
                step(v.tensor_tensor_scan(relsum[r], notstart[:, :], relf[r], 0.0, ALU.mult, ALU.add))
                step(v.tensor_tensor_scan(back[:, ::-1], nextsame[:, ::-1], relf[r][:, ::-1], 0.0, ALU.mult, ALU.add))
                step(v.tensor_copy(lastf[:, 0, r:r + 1], relsum[r][:, COLS - 1:COLS]))
                step(v.tensor_copy(lastf[:, 1, r:r + 1], back[:, 0:1]))
                step(v.tensor_tensor(relsum[r], relsum[r], back, ALU.add))
            v.memset(weight[:, :], 0.0).then_inc(ends_counted, 1)
            dve.wait_ge(ends_counted, 1)
            dve.wait_ge(pre_pe, 2)
            step(v.tensor_copy(inout.rearrange("p a b -> p (a b)"), ps[:, 7, 0:2 * REL]))
            for r in range(REL):
                step(v.scalar_tensor_tensor(out=back, in0=isfirst, scalar=inout[:, 0, r:r + 1], in1=relsum[r],
                                            op0=ALU.mult, op1=ALU.add))
                step(v.scalar_tensor_tensor(out=total, in0=islast, scalar=inout[:, 1, r:r + 1], in1=back,
                                            op0=ALU.mult, op1=ALU.add))
                step(v.scalar_tensor_tensor(out=back, in0=total, scalar=-1.0, in1=relf[r], op0=ALU.add, op1=ALU.mult))
                step(v.tensor_tensor(weight[:, :], weight[:, :], back, ALU.add))
            step(v.tensor_scalar(weight[:, :], weight[:, :], 1.0, None, ALU.max))
            step(v.reciprocal(weight[:, :], weight[:, :]))
            dve.wait_ge(pre_dma, 16 * 11)

            def over_t(a, c):
                return a.unsqueeze(2).broadcast_to([NP, NT, c])

            def over_c(b, n, c):
                return b.unsqueeze(1).broadcast_to([NP, n, c])

            n_sqrt = [0]

            def root(from_):
                from_.then_inc(to_sqrt, 1)
                n_sqrt[0] += 1
                dve.wait_ge(sqrt_done, n_sqrt[0])
                step(v.reciprocal(stat[:, 1, :], stat[:, 3, :]))

            def layernorm(y, square=None):
                sq = tmp[:, :, 32:48] if square is None else square
                step(v.tensor_reduce(stat[:, 0, :], y, AX_X, ALU.add))
                step(v.tensor_scalar(stat[:, 0, :], stat[:, 0, :], 1.0 / 16, None, ALU.mult))
                step(v.tensor_tensor(y, y, over_t(stat[:, 0, :], 16), ALU.subtract))
                step(v.tensor_tensor(sq, y, y, ALU.mult))
                step(v.tensor_reduce(stat[:, 0, :], sq, AX_X, ALU.add))
                root(v.tensor_scalar(stat[:, 2, :], stat[:, 0, :], 1.0 / 16, EPS, ALU.mult, ALU.add))
                step(v.tensor_tensor(X[:, :, :], y, over_t(stat[:, 1, :], 16), ALU.mult))

            def flat(C, a):
                return a.rearrange("p a b -> p (a b)")[:, 0:NT * C].rearrange("p (t c) -> p t c", c=C)

            def finish_sums(st, C):
                a = flat(C, agg)
                dve.wait_ge(agg_gathered, 16 * NT * (st + 1))
                step(v.tensor_tensor(a, a, over_t(has[:, :], C), ALU.mult))
                dve.wait_ge(spans_summed, st + 1)
                for t0, n, piece in dense_all(6, C):
                    step(v.tensor_tensor(a[:, t0:t0 + n, :], a[:, t0:t0 + n, :], piece, ALU.add))
                return a

            def add_dense(d, y, bank, width, other=None):
                dve.wait_ge(dense_done, d + 1)
                for t0, n, piece in dense_all(bank, width):
                    step(v.tensor_tensor(y[:, t0:t0 + n, :], (y if other is None else other)[:, t0:t0 + n, :], piece, ALU.add))

            def edge_sums(st, C, kind):
                taken = st if st < 2 else st - DEPTH
                sin = scan_in.rearrange("p a b -> p (a b)")[:, 0:C * (CH + 1)]
                sfl = scan_flag.rearrange("p a b -> p (a b)")[:, 0:C * (CH + 1)]
                sout = scan_out.rearrange("p a b -> p (a b)")[:, 0:C * (CH + 1)]
                sin3, sfl3, sout3 = (a.rearrange("p (c u) -> p c u", u=CH + 1) for a in (sin, sfl, sout))
                q0 = NCH * PAIRS * (st - 2)
                k0 = NCH * st
                step(v.memset(sfl3[:, :, 0:1], 0.0))
                v.memset(sin3[:, :, 0:1], 0.0).then_inc(carried, 1)

                def body(k, s):
                    r = rows[s].rearrange("p a b -> p (a b)")[:, 0:CH * C].rearrange("p (u c) -> p u c", c=C)
                    o = scanned_rows[s].rearrange("p a b -> p (a b)")[:, 0:CH * C].rearrange("p (u c) -> p u c", c=C)
                    flags = notstart[:, :].rearrange("p (k u) -> p k u", u=CH)[:, k, :]
                    if not isinstance(k, int) or k0 + k >= 1:
                        dve.wait_ge(scanned, k + k0)
                    v.tensor_scalar(sfl3[:, :, 1:CH + 1], flags.unsqueeze(1).broadcast_to([P, C, CH]), 1.0, None,
                                    ALU.mult).then_inc(flags_made, 1)
                    if kind == "mlp":
                        dve.wait_ge(gathered[s], half(k) * (16 * CH) + (16 * CH * ((HALF + 1) if s == 0 else HALF) * st + 16 * CH))
                        for i in range(PAIRS + 1):
                            b = (PAIRS * s + i) % 2
                            if i < PAIRS:
                                q = k * PAIRS + i
                                dve.wait_ge(w_ready, q + (q0 + 1))
                                if not isinstance(q, int) or q0 + q >= 2:
                                    dve.wait_ge(reduced, q + (q0 - 1))
                                v.tensor_tensor(prod[b].rearrange("p t (i o) -> p t i o", i=16),
                                                ps[:, b, :].rearrange("p (t i o) -> p t i o", t=2, i=16),
                                                r[:, 2 * i:2 * i + 2, :].unsqueeze(3).broadcast_to([P, 2, 16, 16]),
                                                ALU.mult).then_inc(prod_done, 1)
                            if i:
                                q = k * PAIRS + i - 1
                                dve.wait_ge(prod_done, q + (q0 + 1))
                                v.tensor_reduce(sin3[:, :, 2 * i - 1:2 * i + 1].rearrange("p o t -> p t o"),
                                                prod[1 - b].rearrange("p t (i o) -> p t o i", i=16), AX_X, ALU.add)\
                                    .then_inc(reduced, 1)
                        dve.wait_ge(reduced, k * PAIRS + (q0 + PAIRS))
                    else:
                        dve.wait_ge(gathered[s], half(k) * (16 * CH) + (16 * CH * ((HALF + 1) if s == 0 else HALF) * st + 16 * CH))
                        to = sin3[:, :, 1:CH + 1].rearrange("p c u -> p u c")
                        if kind == "weighted":
                            w = weight[:, :].rearrange("p (k u) -> p k u", u=CH)[:, k, :]
                            v.tensor_tensor(to, r, w.unsqueeze(2).broadcast_to([P, CH, C]), ALU.mult).then_inc(rows_taken, 1)
                        else:
                            v.tensor_copy(to, r).then_inc(rows_taken, 1)
                        dve.wait_ge(rows_taken, k + (NCH * taken + 1))
                    dve.wait_ge(flags_made, k + (k0 + 1))
                    dve.wait_ge(carried, k + (k0 + st + 1))
                    if not isinstance(k, int) or k0 + k >= 1:
                        dve.wait_ge(rows_scanned, k + k0)
                    v.tensor_tensor_scan(sout, sfl, sin, 0.0, ALU.mult, ALU.add).then_inc(scanned, 1)
                    dve.wait_ge(scanned, k + (k0 + 1))
                    v.tensor_copy(sin3[:, :, 0:1], sout3[:, :, CH:CH + 1]).then_inc(carried, 1)
                    sb0 = 16 * ((HALF + 1) if s == 0 else HALF) * st
                    if not isinstance(k, int) or k >= 2 or st:
                        dve.wait_ge(stored[s], half(k) * 16 + sb0)
                    v.tensor_copy(o, sout3[:, :, 1:CH + 1].rearrange("p c u -> p u c")).then_inc(rows_scanned, 1)

                over_chunks(dve, body)
                dve.wait_ge(carried, k0 + NCH + st + 1)

            root(v.tensor_scalar(stat[:, 2, :], deg[:, :], 1.0, None, ALU.add))
            step(v.tensor_copy(dinv[:, :], stat[:, 1, :]))
            f16 = feat[:, :, 0:16]
            v.tensor_tensor(f16, X[:, :, :], over_t(dinv[:, :], 16), ALU.mult).then_inc(table_ready, 1)
            edge_sums(0, 16, "plain")
            a = finish_sums(0, 16)
            step(v.tensor_tensor(a, a, f16, ALU.add))
            dve.wait_ge(table_written, 16)
            v.tensor_tensor(f16, a, over_t(dinv[:, :], 16), ALU.mult).then_inc(feat_ready, 1)
            add_dense(0, tmp[:, :, 0:48], 2, 48, other=b1s[:, :].unsqueeze(1).broadcast_to([NP, NT, 48]))
            v.tensor_scalar(feat[:, :, 0:48], tmp[:, :, 0:48], 0.0, None, ALU.max).then_inc(feat_ready, 1)
            dve.wait_ge(dense_done, 2)
            f32_ = feat[:, :, 0:32]
            for t0, n, piece in dense_all(2, 32):
                m = v.tensor_tensor(f32_[:, t0:t0 + n, :], piece, over_t(dinv[:, :], 32)[:, t0:t0 + n, :], ALU.mult)
                if t0 + n < NT:
                    step(m)
            m.then_inc(table_ready, 1)
            if upto <= 1:
                return
            edge_sums(1, 32, "plain")
            a = finish_sums(1, 32)
            step(v.tensor_tensor(a, a, f32_, ALU.add))
            step(v.tensor_tensor(a, a, over_t(dinv[:, :], 32), ALU.mult))
            step(v.tensor_tensor(a, a, over_c(b2s[:, :], NT, 32), ALU.add))
            dve.wait_ge(table_written, 32)
            v.tensor_scalar(f32_, a, 0.0, None, ALU.max).then_inc(feat_ready, 1)
            add_dense(2, tmp[:, :, 0:16], 2, 16, other=over_c(bfcs[:, :], NT, 16))
            step(v.tensor_tensor(tmp[:, :, 0:16], tmp[:, :, 0:16], X[:, :, :], ALU.add))
            layernorm(tmp[:, :, 0:16])
            step(v.tensor_copy(nodes[:, :, :], X[:, :, :]))
            for d in range(DEPTH):
                st = 2 + d
                if upto <= st:
                    break
                step(v.memset(stat[:, 0, :], 0.0))
                v.memset(stat[:, 1, :], 0.0).then_inc(table_ready, 1)
                v.memset(stat[:, 2, :], 0.0).then_inc(feat_ready, 1)
                edge_sums(st, 16, "mlp")
                a = finish_sums(st, 16)
                step(v.tensor_tensor(a, a, over_t(inv_deg[:, :], 16), ALU.mult))
                step(v.tensor_tensor(a, a, over_c(rootbs[:, d, :], NT, 16), ALU.add))
                dve.wait_ge(dense_done, 4 + d)
                dve.wait_ge(table_written, 16 * (st + 1))
                v.tensor_tensor(tmp[:, :, 0:16], a, ps[0:NP, 7, 0:NT * 16].rearrange("p (t c) -> p t c", c=16),
                                ALU.add).then_inc(to_gelu, 1)
                dve.wait_ge(gelu_done, d + 1)
            if upto > 5:
                step(v.tensor_tensor(tmp[:, :, 0:16], nodes[:, :, :], X[:, :, :], ALU.add))
                layernorm(tmp[:, :, 0:16])
            if upto > 6:
                step(v.memset(stat[:, 0, :], 0.0))
                v.memset(stat[:, 1, :], 0.0).then_inc(table_ready, 1)
                v.memset(stat[:, 2, :], 0.0).then_inc(feat_ready, 1)
                edge_sums(6, 32, "weighted")
                a = finish_sums(6, 32)
                step(v.tensor_tensor(a, a, over_c(Rb1s[:, :], NT, 32), ALU.add))
                add_dense(7, a, 4, 32)
                dve.wait_ge(table_written, 16 * 7)
                step(v.tensor_scalar(feat[:, :, 0:32], a, 0.0, None, ALU.max))
                v.memset(stat[:, 1, :], 0.0).then_inc(table_ready, 1)
                v.memset(stat[:, 2, :], 0.0).then_inc(feat_ready, 1)
            if upto > 7:
                edge_sums(7, 16, "weighted")
                a = finish_sums(7, 16)
                step(v.tensor_tensor(a, a, over_c(Rb2s[:, :], NT, 16), ALU.add))
                add_dense(8, a, 4, 16)
                step(v.tensor_tensor(tmp[:, :, 0:16], a, X[:, :, :], ALU.add))
                layernorm(tmp[:, :, 0:16])
            U = J3 + 1
            n3, p3, d3 = (a.rearrange("p (c u) -> p c u", u=U) for a in (attn_neg, peak, decay))
            e3 = [scores[s][:, 0, :].rearrange("p (c u) -> p c u", u=U) for s in range(2)]
            t3 = [scores[s][:, 1, :].rearrange("p (c u) -> p c u", u=U) for s in range(2)]
            step(v.memset(n3[:, :, 0:1], -BIG))
            step(v.memset(d3[:, :, 0:1], 0.0))
            step(v.memset(p3[:, :, J3:U], 0.0))
            step(v.memset(e3[1][:, :, J3:U], 0.0))
            step(v.memset(t3[1][:, :, J3:U], 0.0))
            step(v.tensor_copy(nodes[:, :, :], X[:, :, :]))
            step(v.memset(zeros, 0.0))
            v.memset(stat[:, 0, :], 0.0).then_inc(zeros_made, 1)
            v.memset(stat[:, 1, :], 0.0).then_inc(tail_ready, 1)
            v.memset(stat[:, 2, :], 0.0).then_inc(table_ready, 1)

            def score(k, s):
                dve.wait_ge(x_gathered[s], half(k) * (16 * J3) + 16 * J3)
                if not known(k) or k >= 2:
                    dve.wait_ge(rows_made, k * 3 - 3)
                for u in range(J3):
                    dve.wait_ge(wa_ready, k * J3 + (u + 1))
                    to = scores[s].rearrange("p a (i o u) -> p a i o u", i=16, o=16)[:, :, :, :, u + 1]
                    x_ = xrows[s][:, u * 16:(u + 1) * 16].unsqueeze(1).unsqueeze(3).broadcast_to([P, 2, 16, 16])
                    v.tensor_tensor(to, ps[:, u % 7, :].rearrange("p (a i o) -> p a i o", a=2, i=16), x_,
                                    ALU.mult).then_inc(scored, 1)

            def attend(k, s):
                v.tensor_copy(e3[s][:, :, 0:1], p3[:, :, J3:U]).then_inc(carries, 1)
                v.tensor_copy(t3[s][:, :, 0:1], t3[1 - s][:, :, J3:U]).then_inc(carries, 1)
                dve.wait_ge(carries, k * 3 + 2)
                dve.wait_ge(scored, k * J3 + J3)
                dve.wait_ge(neg_made, k + 1)
                if not known(k) or k >= 1:
                    dve.wait_ge(rows_made, k * 3 - 2)
                v.tensor_tensor_scan(peak, attn_neg, scores[s][:, 0, :], 0.0, ALU.add, ALU.max).then_inc(peaked, 1)
                dve.wait_ge(peaked, k + 1)
                v.tensor_copy(e3[s][:, :, 0:1], e3[1 - s][:, :, J3:U]).then_inc(carries, 1)
                v.tensor_tensor(e3[s][:, :, 1:U], e3[s][:, :, 1:U], p3[:, :, 1:U], ALU.subtract).then_inc(risen, 1)
                dve.wait_ge(carries, k * 3 + 3)
                if not known(k) or k + 1 < N3:
                    score(k + 1, 1 - s)
                dve.wait_ge(decay_begun, k + 1)
                v.tensor_tensor(d3[:, :, 1:U], d3[:, :, 1:U], p3[:, :, 1:U], ALU.subtract).then_inc(decayed, 1)
                dve.wait_ge(risen_exp, k + 1)
                v.tensor_tensor(t3[s][:, :, 1:U], t3[s][:, :, 1:U], e3[s][:, :, 1:U], ALU.mult).then_inc(weighted_msg, 1)
                dve.wait_ge(weighted_msg, k + 1)
                dve.wait_ge(decay_exp, k + 1)
                v.tensor_tensor_scan(scores[s][:, 0, :], decay, scores[s][:, 0, :], 0.0, ALU.mult, ALU.add).then_inc(den_done, 1)
                v.tensor_tensor_scan(scores[s][:, 1, :], decay, scores[s][:, 1, :], 0.0, ALU.mult, ALU.add).then_inc(num_done, 1)
                dve.wait_ge(den_done, k + 1)
                dve.wait_ge(num_done, k + 1)

            score(0, 0)
            over_chunks3(dve, attend)
            dve.wait_ge(rows_made, 3 * N3)
            dve.wait_ge(tail_pe, 1)
            for q in range(3):
                step(v.tensor_copy(lastT[:, q, :], ps[:, q, 0:2 * P]))
            step(v.tensor_copy(chainT.rearrange("p (a b) -> p a b", a=2), chain[:, :].unsqueeze(1).broadcast_to([P, 2, P])))
            step(v.tensor_tensor_scan(peakT, chainT, lastT[:, 0, :], 0.0, ALU.add, ALU.max))
            v.tensor_tensor(riseT, lastT[:, 0, :], peakT, ALU.subtract).then_inc(tail_dve, 1)
            step(v.memset(decT, -BIG))
            cT, kT, xT = (a.rearrange("p (a b) -> p a b", a=2) for a in (chainT, peakT, decT))
            step(v.tensor_tensor(xT[:, :, 1:P], cT[:, :, 1:P], kT[:, :, 0:P - 1], ALU.add))
            v.tensor_tensor(xT[:, :, 1:P], xT[:, :, 1:P], kT[:, :, 1:P], ALU.subtract).then_inc(tail_dve, 1)
            dve.wait_ge(tail_act, 2)
            step(v.tensor_tensor(denT, lastT[:, 1, :], riseT, ALU.mult))
            step(v.tensor_tensor(numT, lastT[:, 2, :], riseT, ALU.mult))
            step(v.tensor_tensor_scan(lastT[:, 1, :], decT, denT, 0.0, ALU.mult, ALU.add))
            step(v.tensor_tensor_scan(lastT[:, 2, :], decT, numT, 0.0, ALU.mult, ALU.add))
            step(v.memset(shiftT, 0.0))
            for q, a in enumerate((peakT, lastT[:, 1, :], lastT[:, 2, :])):
                step(v.tensor_copy(shiftT[:, q, :].rearrange("p (a b) -> p a b", a=2)[:, :, 1:P + 1],
                                   a.rearrange("p (a b) -> p a b", a=2)))
            v.memset(own, 0.0).then_inc(own_cleared, 1)
            v.memset(both, 0.0).then_inc(shift_made, 1)
            dve.wait_ge(tail_gather, 16)
            dve.wait_ge(tail_pe, 2)
            for q in range(3):
                step(v.tensor_copy(cin[:, q, :], ps[:, 3 + q, 0:2 * P]))
            step(v.tensor_tensor(both[:, 0:CC], own[:, 0:CC], cin[:, 0, :], ALU.max))
            v.tensor_tensor(ea_, own[:, 0:CC], both[:, 0:CC], ALU.subtract).then_inc(tail_dve, 1)
            v.tensor_tensor(eb_, cin[:, 0, :], both[:, 0:CC], ALU.subtract).then_inc(tail_dve, 1)
            dve.wait_ge(tail_act, 4)
            for q in (1, 2):
                o_ = own[:, q * CC:(q + 1) * CC]
                step(v.tensor_tensor(o_, o_, ea_, ALU.mult))
                step(v.tensor_tensor(cin[:, q, :], cin[:, q, :], eb_, ALU.mult))
                step(v.tensor_tensor(both[:, q * CC:(q + 1) * CC], o_, cin[:, q, :], ALU.add))
            v.memset(stat3[:, :], 0.0).then_inc(fixed, 1)
            dve.wait_ge(tail_dma, 16)
            step(v.tensor_scalar(nohas, has[:, :], -1.0, 1.0, ALU.mult, ALU.add))
            den, num = node_att[:, :, 0:CC], node_att[:, :, CC:2 * CC]
            step(v.tensor_tensor(den, den, over_t(nohas, CC), ALU.add))
            step(v.reciprocal(den, den))
            step(v.tensor_tensor(num, num, den, ALU.mult))
            step(v.tensor_reduce(summed, num.rearrange("p t (i o) -> p t o i", i=16), AX_X, ALU.add))
            step(v.tensor_tensor(summed, summed, nodes[:, :, :], ALU.add))
            layernorm(summed, summed2)
            v.memset(stat3[:, :], 0.0).then_inc(out_done, 1)


_INS = ["x", "src", "dst", "dst_ends", "edge_type_8", "eaT", "efT", "L0_gnn_W1", "L0_gnn_b1", "L0_gnn_W2", "L0_gnn_b2",
        "L0_gnn_Wfc", "L0_gnn_bfc", "L1_gnn_kW1", "L1_gnn_kb1", "L1_gnn_kW2", "L1_gnn_kb2", "L1_gnn_kW3",
        "L1_gnn_kb3", "L1_gnn_root_W", "L1_gnn_root_b", "L2_gnn_W1", "L2_gnn_root1", "L2_gnn_b1", "L2_gnn_W2",
        "L2_gnn_root2", "L2_gnn_b2", "L3_gnn_W_msg", "L3_gnn_b_msg", "L3_gnn_W_attn", "L3_gnn_b_attn"]


def kernel(**inputs):
    import numpy as _np
    import concourse.bacc as _bacc
    from concourse.bass_utils import run_bass_kernel_spmd as _run

    a = {k: _np.asarray(v) for k, v in inputs.items()}
    pad = P * COLS - E

    def edges(v, fill):
        tail = _np.full((pad,) + v.shape[1:], fill, v.dtype)
        return _np.concatenate([v, tail]).reshape((P, COLS) + v.shape[1:])

    a["src"], a["dst"], a["edge_type_8"] = edges(a["src"], 0), edges(a["dst"], N), edges(a["edge_type_8"], 0)
    a["dst_ends"] = _np.stack([a["dst"][:, 0], a["dst"][:, -1]])
    a["eaT"] = edges(a["edge_attr_6"], 0).transpose(2, 1, 0).reshape(6, COLS * P)
    a["efT"] = edges(a["edge_attr_16"], 0).transpose(2, 1, 0).reshape(16, COLS * P)
    a["efT"] = _np.concatenate([a["efT"], _np.ones((1, COLS * P), a["efT"].dtype)])
    nc = _bacc.Bacc("TRN2", target_bir_lowering=False, num_devices=1)
    arrays, args = {}, []
    for name in _INS:
        v = _np.ascontiguousarray(a[name])
        arrays["in_" + name] = v
        args.append(nc.dram_tensor("in_" + name, v.shape, mybir.dt.from_np(v.dtype), kind="ExternalInput").ap())
    out = nc.dram_tensor("out_0", (N, LAT), F32, kind="ExternalOutput").ap()
    build(nc, *args, out)
    r = _run(nc, [arrays], core_ids=[0])
    return r.results[0]["out_0"]
```

```python
from contextlib import ExitStack

import concourse.bass as bass
from concourse import mybir

F32 = mybir.dt.float32
F16 = mybir.dt.float16
BF16 = mybir.dt.bfloat16
I32 = mybir.dt.int32
ALU = mybir.AluOpType
ACT = mybir.ActivationFunctionType
AX_X = mybir.AxisListType.X

P = 128
N, E, LAT = 3125, 103125, 16
NP, NT = 125, 25
COLS = -(-E // P)
CH = 26
NCH = COLS // CH
HALF = NCH // 2
PAIRS = CH // 2
REL = 8
KD = 128
DEPTH = 4
EPS = 1e-5
BIG = 3.0e38
SKIP = 4096
J3 = 13
N3 = COLS // J3
CC = 256
STAGES = [("gcn1", 16, "plain"), ("gcn2", 32, "plain")] + [(f"nnconv{i}", 16, "mlp") for i in range(DEPTH)] \
    + [("rgcn1", 32, "weighted"), ("rgcn2", 16, "weighted")]
NEAR, FAR = 5, 5
BLOCK = NEAR * P
PICK = {"gcn1": (10, 2), "gcn2": (12, 4)}
PICK.update({f"nnconv{i}": (8, 2) for i in range(DEPTH)})
MAXPICK = max(m for m, _ in PICK.values())
assert BLOCK * FAR >= N
assert NP * NT == N and NCH * CH == COLS and N3 * J3 == COLS and NCH % 2 == 1


def over_chunks(eng, body):
    body(0, 0)
    body(1, 1)
    with eng.Fori(1, HALF - 1) as turn:
        body(turn * 2, 0)
        body(turn * 2 + 1, 1)
    body(NCH - 3, 0)
    body(NCH - 2, 1)
    body(NCH - 1, 0)


def over_chunks3(eng, body):
    body(0, 0)
    body(1, 1)
    with eng.Fori(1, N3 // 2 - 1) as turn:
        body(turn * 2, 0)
        body(turn * 2 + 1, 1)
    body(N3 - 2, 0)
    body(N3 - 1, 1)


H_RING, W_RING = 3, 4
W_BANKS = (0, 1, 4, 5)
H1_BANKS, H2_BANKS = (2, 3, 6), (4, 5, 7)


def ring(size, s, i):
    while i < 0:
        i, s = i + PAIRS, 1 - s
    return (i + s * (PAIRS % size)) % size


def ago(size, s, i):
    b = 1
    while ring(size, s, i - b) != ring(size, s, i):
        b += 1
    return b


def known(k):
    return isinstance(k, int)


def half(k):
    return k // 2


def build(nc, x, src, srcT, dst, ends, etype, eaT, efT, W1, b1, W2, b2, Wfc, bfc, kW1, kb1, kW2, kb2, kW3, kb3,
          rootW, rootb, RW1, Rroot1, Rb1, RW2, Rroot2, Rb2, Wm, bm, Wa, ba, out):
    with ExitStack() as ctx:
        def sb(name, shape, dt=F32):
            return ctx.enter_context(nc.sbuf_tensor(name, shape, dt))

        def sem(name):
            return ctx.enter_context(nc.semaphore(name))

        def dram(name, shape, dt=F32):
            return nc.dram_tensor(name, shape, dt, kind="Internal").ap()

        table16 = dram("table16", [N, 16])
        table32 = dram("table32", [N, 32])
        rel32 = dram("rel32", [N * REL, 32])
        rel16 = dram("rel16", [N * REL, 16])
        sums16 = dram("sums16", [P * COLS, 16])
        sums32 = dram("sums32", [P * COLS, 32])
        dst_rows = dram("dst_rows", [P, COLS])
        end_index = dram("end_index", [P, COLS], I32)
        neg_flags = dram("neg_flags", [P, COLS])
        attn_table = dram("attn_table", [N, 3 * CC])
        pick_index = dram("pick_index", [COLS * P], F16)
        h2_dram = dram("h2_dram", [KD, COLS * P])
        rel_index = dram("rel_index", [P, COLS], I32)
        tables = [table16, table32] + [table16] * DEPTH + [rel32, rel16]
        indices = [src] * (2 + DEPTH) + [rel_index] * 2

        notstart = sb("notstart", [P, COLS])
        weight = sb("weight", [P, COLS])
        ident = sb("ident", [P, P])
        last_edge = sb("last_edge", [NP, NT], I32)
        has = sb("has", [NP, NT])
        deg = sb("deg", [NP, NT])
        dinv = sb("dinv", [NP, NT])
        inv_deg = sb("inv_deg", [NP, NT])
        X = sb("X", [NP, NT, 16])
        nodes = sb("nodes", [NP, NT, 16])
        pace = sb("pace", [1, 2])
        chain = sb("chain", [P, P])
        fix_index = sb("fix_index", [P, 1], I32)
        end_of = sb("end_of", [P, 2, J3], I32)

        W1s = sb("W1s", [16, 48]); W2s = sb("W2s", [48, 32]); Wfcs = sb("Wfcs", [32, 16])
        b1s = sb("b1s", [NP, 48]); b2s = sb("b2s", [NP, 32]); bfcs = sb("bfcs", [NP, 16])
        kW1s = sb("kW1s", [6, KD]); kW2s = sb("kW2s", [KD, KD]); kW3s = sb("kW3s", [KD, CC])
        kb1s = sb("kb1s", [KD, 1]); kb2s = sb("kb2s", [KD, 1])
        kb3s = sb("kb3s", [1, CC]); kb3p = sb("kb3p", [1, 3, CC], BF16); kb3r = sb("kb3r", [1, 2, CC])
        kb3w = sb("kb3w", [3, 2, CC], BF16)
        ones3 = sb("ones3", [3, P], BF16)
        rootWs = sb("rootWs", [16, DEPTH, 16]); rootbs = sb("rootbs", [NP, DEPTH, 16])
        RW1s = sb("RW1s", [16, REL, 32]); Rroot1s = sb("Rroot1s", [16, 32]); Rb1s = sb("Rb1s", [NP, 32])
        RW2s = sb("RW2s", [32, REL, 16]); Rroot2s = sb("Rroot2s", [32, 16]); Rb2s = sb("Rb2s", [NP, 16])

        index = sb("index", [P, 2, CH], I32)
        ARENA = 40700
        pick_mask = sb("pick_mask", [P, COLS, FAR], BF16)
        neg_lanes = sb("neg_lanes", [P, NEAR])
        lanes = sb("lanes", [P, NEAR])
        arena = sb("arena", [P, ARENA + N])
        spans = arena[:, ARENA:ARENA + N]
        limit = [ARENA]
        at = [0]

        def carve(parts, *shape, dt=F32):
            n = 1
            for d in shape:
                n *= d
            full = n
            if dt in (BF16, F16):
                n = (n + 1) // 2
            v = arena[0:parts, at[0]:at[0] + n]
            at[0] += n
            assert at[0] <= limit[0], at[0]
            if dt != F32:
                v = v.bitcast(dt)
                v = v[:, 0:full]
            if len(shape) == 2:
                v = v.rearrange("p (a b) -> p a b", a=shape[0])
            if len(shape) == 3:
                v = v.rearrange("p (a b c) -> p a b c", a=shape[0], b=shape[1])
            return v

        rows = [carve(P, CH, 32) for _ in range(2)]
        scan_in = carve(P, 32, CH + 1)
        scan_flag = carve(P, 32, CH + 1)
        scan_out = carve(P, 32, CH + 1)
        scanned_rows = [carve(P, CH, 32) for _ in range(2)]
        h1s = [carve(KD, 2 * P) for _ in range(H_RING)]
        shared = at[0]
        ysb = carve(NP, NT, CC)
        at[0] = shared
        h2s = [carve(KD, CH * P) for _ in range(2)]
        hot = [carve(P, NEAR, MAXPICK * P, dt=BF16) for _ in range(2)]
        table_f = carve(P, FAR * NEAR, 32)
        table_r = carve(P, FAR * NEAR, 32)
        table_p = [carve(P, FAR * NEAR, 32, dt=BF16) for _ in range(3)]
        pick_in = [carve(P, MAXPICK * P, dt=F16) for _ in range(2)]
        kept = [carve(P, 480) for _ in range(2)]
        feat = carve(NP, NT, 48)
        shared = at[0]
        prod = [carve(P, 2, CC) for _ in range(3)]
        agg = carve(NP, NT, 32)
        tmp = carve(NP, NT, 48)
        featT = carve(48, N)
        far_off = [carve(P, MAXPICK * P, dt=BF16) for _ in range(2)]
        rest_ = at[0]
        at[0] = shared
        eaTs = [carve(6, CH * P) for _ in range(2)]
        at[0] = rest_
        stat = sb("stat", [NP, 4, NT]); stat3 = sb("stat3", [1, 1])
        at[0] = 0
        dsti = carve(P, COLS, dt=I32)
        dstf = carve(P, COLS)
        typei = carve(P, COLS, dt=I32)
        typef = carve(P, COLS)
        nextsame = carve(P, COLS)
        relf = [carve(P, COLS) for _ in range(REL)]
        relsum = [carve(P, COLS) for _ in range(REL)]
        back = carve(P, COLS)
        total = carve(P, COLS)
        isfirst = carve(P, COLS)
        islast = carve(P, COLS)
        idxf = carve(P, COLS)
        srci = carve(P, COLS, dt=I32); srcTi = carve(P, COLS, dt=I32)
        far = carve(P, COLS); srcTf = carve(P, COLS); pick_f16 = carve(P, COLS, dt=F16)
        iota_n = carve(P, N + 1, dt=I32)
        node_row = carve(P, N + 1)
        edge_rows = [carve(NP, COLS) for _ in range(2)]
        hits = carve(NP, COLS); hits_n = carve(P, N + 1)
        small = carve(P, 64)
        firstrow_i = carve(P, P, dt=I32); lastrow_i = carve(P, P, dt=I32)
        firstrow = carve(P, P); lastrow = carve(P, P)
        colno = carve(P, P)
        intake = carve(P, P); intake2 = carve(P, P)
        nexti = carve(P, 1, dt=I32)
        part_i = carve(P, 1, dt=I32)
        want_i = carve(NP, NT + 1, dt=I32); want = carve(NP, NT + 1)
        rowno_f = carve(NP, NT + 1); rowno = carve(NP, NT + 1, dt=I32)
        lower = carve(NP, NT + 1)
        lastf = carve(P, 2, REL)
        inout = carve(P, 2, REL)
        nodeq = carve(NP, NT); nodeq2 = carve(NP, NT); nodeq3 = carve(NP, NT)
        endf = carve(P, COLS); endi = carve(P, COLS, dt=I32); negf = carve(P, COLS)
        prevlast_row = carve(P, P); wholerow = carve(P, P)
        at[0] = 0
        limit[0] = ARENA + N
        scores = [carve(P, 2, CC * (J3 + 1)) for _ in range(2)]
        decay = carve(P, CC * (J3 + 1))
        attn_neg = carve(P, CC * (J3 + 1))
        peak = [carve(P, CC * (J3 + 1)) for _ in range(2)]
        AFTER_PEAK = at[0]
        end_rows = carve(P, J3, 3 * CC)
        xrows = [carve(P, J3 * 16) for _ in range(2)]
        efTs = [carve(17, J3 * P) for _ in range(2)]
        zeros = carve(NP, 3 * CC)
        neg_in = [carve(P, J3) for _ in range(2)]
        Wcat = carve(17, 2, CC)
        at[0] = 0
        lastT = carve(P, 3, 2 * P)
        chainT = carve(P, 2 * P); peakT = carve(P, 2 * P); decT = carve(P, 2 * P); riseT = carve(P, 2 * P)
        denT = carve(P, 2 * P); numT = carve(P, 2 * P)
        shiftT = carve(P, 3, 2 * (P + 1))
        cin = carve(P, 3, CC); own = carve(P, 3 * CC); both = carve(P, 3 * CC)
        ea_ = carve(P, CC); eb_ = carve(P, CC)
        assert at[0] <= 2 * CC * (J3 + 1)
        at[0] = AFTER_PEAK
        node_att = carve(NP, NT, 2 * CC)
        nohas = carve(NP, NT)
        at[0] = 2 * CC * (J3 + 1) * 2
        summed = carve(NP, NT, 16); summed2 = carve(NP, NT, 16)
        colfirst, collast, nextfirst, spanval, partno, ones1, spaneq, spanneg = (small[:, i:i + 1] for i in range(8))

        ps = ctx.enter_context(nc.psum_tensor("ps", [P, 8, 512], F32))

        loaded = sem("loaded")
        made = sem("made")
        table_written = sem("table_written")
        index_loaded = [sem(f"index_loaded{s}") for s in range(2)]
        gathered = [sem(f"gathered{s}") for s in range(2)]
        paced = sem("paced")
        rows_taken = sem("rows_taken")
        flags_made = sem("flags_made")
        scanned = sem("scanned")
        carried = sem("carried")
        rows_scanned = sem("rows_scanned")
        stored = [sem(f"stored{s}") for s in range(2)]
        agg_gathered = sem("agg_gathered")
        spans_summed = sem("spans_summed")
        feat_ready = sem("feat_ready")
        transposed = sem("transposed")
        featT_ready = sem("featT_ready")
        dense_done = sem("dense_done")
        y_ready = sem("y_ready")
        y_taken = sem("y_taken")
        table_ready = sem("table_ready")
        to_sqrt = sem("to_sqrt"); sqrt_done = sem("sqrt_done")
        to_gelu = sem("to_gelu"); gelu_done = sem("gelu_done")
        ea_loaded = [sem(f"ea_loaded{s}") for s in range(2)]
        h1_ready = sem("h1_ready"); h1_made = sem("h1_made")
        h2_ready = sem("h2_ready"); h2_made = sem("h2_made")
        w_ready = sem("w_ready"); prod_done = sem("prod_done"); reduced = sem("reduced")
        pickidx_made = sem("pickidx_made"); table_back = sem("table_back"); parts_made = sem("parts_made")
        pick_loaded = [sem(f"pick_loaded{s}") for s in range(2)]
        off_made = sem("off_made"); lanes_made = sem("lanes_made")
        hot_made = sem("hot_made"); picked = sem("picked"); masked = sem("masked"); kept_rows = sem("kept_rows")
        h2_stored = [sem(f"h2_stored{s}") for s in range(2)]; h2_loaded = [sem(f"h2_loaded{s}") for s in range(2)]
        pre_dma = sem("pre_dma"); pre_gather = [sem("pre_gather0"), sem("pre_gather1")]
        nexti_cleared = sem("nexti_cleared"); kb3_split = sem("kb3_split"); dstf_made = sem("dstf_made")
        relidx_made = sem("relidx_made"); rowno_made = sem("rowno_made"); below_made = sem("below_made")
        ends_counted = sem("ends_counted")
        pre_pe = sem("pre_pe"); pre_pe2 = sem("pre_pe2"); pre_pool = sem("pre_pool")
        out_done = sem("out_done")
        L3_loaded = [sem(f"L3_loaded{s}") for s in range(2)]
        end_loaded = [sem(f"end_loaded{s}") for s in range(2)]
        zeroed = sem("zeroed"); zeros_made = sem("zeros_made"); Wcat_loaded = sem("Wcat_loaded")
        x_gathered = [sem(f"x_gathered{s}") for s in range(2)]
        scattered = sem("scattered")
        wa_ready = sem("wa_ready"); scored = sem("scored")
        neg_made = sem("neg_made"); peaked = sem("peaked"); carries = sem("carries")
        found = sem("found"); risen = sem("risen"); clipped = sem("clipped")
        risen_exp = sem("risen_exp"); decay_exp = sem("decay_exp")
        index3_loaded = [sem(f"index3_loaded{s}") for s in range(2)]
        weighted_msg = sem("weighted_msg"); den_done = sem("den_done"); num_done = sem("num_done")
        rows_made = sem("rows_made")
        tail_pe = sem("tail_pe"); tail_dve = sem("tail_dve"); tail_act = sem("tail_act"); tail_dma = sem("tail_dma")
        tail_gather = sem("tail_gather"); tail_scatter = sem("tail_scatter"); tail_ready = sem("tail_ready")
        shift_made = sem("shift_made"); own_cleared = sem("own_cleared"); fixed = sem("fixed")
        endidx_made = sem("endidx_made"); negf_made = sem("negf_made")

        DENSE = [(16, [(W1s[:, :], 48, 2)]), (48, [(W2s[:, :], 32, 2)]), (32, [(Wfcs[:, :], 16, 2)])] \
            + [(16, [(rootWs[:, i, :], 16, 7)]) for i in range(DEPTH)] \
            + [(16, [(Rroot1s[:, :], 32, 4)]), (32, [(Rroot2s[:, :], 16, 4)])]
        REL_W = {7: (RW1s[:, :, :].rearrange("p r c -> p (r c)"), 256), 8: (RW2s[:, :, :].rearrange("p r c -> p (r c)"), 128)}
        GROUP = 4
        NG = -(-NT // GROUP)

        def dense_out(bank, width, t):
            per = 512 // width
            return ps[0:NP, bank + t // per, (t % per) * width:(t % per + 1) * width]

        def dense_all(bank, width):
            per = 512 // width
            for t0 in range(0, NT, per):
                n = min(per, NT - t0)
                yield t0, n, ps[0:NP, bank + t0 // per, 0:n * width].rearrange("p (t c) -> p t c", c=width)

        block = ctx.enter_context(nc.Block())

        def span_bank(width):
            return 6

        def gather_base(st):
            cols = sum(CH - PICK.get(STAGES[i][0], (0, 0))[0] for i in range(st))
            return [16 * cols * (HALF + 1), 16 * cols * HALF]

        def pick_groups(st):
            m, groups = PICK[STAGES[st][0]]
            per = m // groups
            return [(g, CH - m + g * per, per, (2 if STAGES[st][2] == "mlp" else 0) + g) for g in range(groups)]

        def groups_before(st):
            return NCH * sum(PICK.get(STAGES[i][0], (0, 0))[1] for i in range(st))

        LOADS = [
            (dsti[:, :], dst), (typei[:, :], etype), (srci[:, :], src), (srcTi[:, :], srcT),
            (firstrow_i[:, :], ends[0:1, :].broadcast_to([P, P])),
            (lastrow_i[:, :], ends[1:2, :].broadcast_to([P, P])),
            (X[:, :, :], x.rearrange("(p t) c -> p t c", t=NT)),
            (W1s[:, :], W1), (W2s[:, :], W2), (Wfcs[:, :], Wfc),
            (kW1s[:, :], kW1), (kW2s[:, :], kW2), (kW3s[:, :], kW3),
            (kb1s[:, :], kb1.rearrange("(p a) -> p a", a=1)), (kb2s[:, :], kb2.rearrange("(p a) -> p a", a=1)),
            (kb3s[:, :], kb3.rearrange("(a n) -> a n", a=1)),
            (rootWs[:, :, :], rootW.rearrange("d i o -> i d o")),
            (RW1s[:, :, :], RW1.rearrange("r i o -> i r o")), (RW2s[:, :, :], RW2.rearrange("r i o -> i r o")),
            (Rroot1s[:, :], Rroot1), (Rroot2s[:, :], Rroot2),
            (b1s[:, :], b1.rearrange("(a n) -> a n", a=1).broadcast_to([NP, 48])),
            (b2s[:, :], b2.rearrange("(a n) -> a n", a=1).broadcast_to([NP, 32])),
            (bfcs[:, :], bfc.rearrange("(a n) -> a n", a=1).broadcast_to([NP, 16])),
            (Rb1s[:, :], Rb1.rearrange("(a n) -> a n", a=1).broadcast_to([NP, 32])),
            (Rb2s[:, :], Rb2.rearrange("(a n) -> a n", a=1).broadcast_to([NP, 16])),
            (rootbs[:, :, :].rearrange("p d o -> p (d o)"),
             rootb.rearrange("(a d) o -> a (d o)", a=1).broadcast_to([NP, DEPTH * 16])),
        ]

        @block.sync
        def _(sp):
            for to, frm in LOADS:
                sp.dma_start(to, frm).then_inc(loaded, 16)
            sp.wait_ge(nexti_cleared, 1)
            sp.dma_start(nexti[0:P - 1, :], ends[0:1, 1:P].rearrange("a p -> p a")).then_inc(pre_dma, 16)
            sp.wait_ge(kb3_split, 1)
            for i in range(3):
                for j in range(2):
                    sp.dma_start(kb3w[i:i + 1, j, :], kb3p[0:1, i, :]).then_inc(pre_dma, 16)
            sp.wait_ge(dstf_made, 1)
            sp.dma_start(dst_rows, dstf[:, :]).then_inc(pre_dma, 16)
            sp.wait_ge(relidx_made, 1)
            sp.dma_start(rel_index, srci[:, :]).then_inc(pre_dma, 16)

            sp.wait_ge(endidx_made, 1)
            sp.dma_start(end_index, endi).then_inc(pre_dma, 16)
            sp.wait_ge(negf_made, 1)
            sp.dma_start(neg_flags, negf).then_inc(pre_dma, 16)
            sp.wait_ge(pickidx_made, 1)
            sp.dma_start(pick_index.rearrange("(p j) -> p j", p=P), pick_f16).then_inc(pre_dma, 16)
            sp.wait_ge(pre_dma, 16 * 12)

            for st, (name, C, kind) in enumerate(STAGES):
                sums = sums16 if C == 16 else sums32
                sums_v = sums.rearrange("(p k u) c -> p k (u c)", k=NCH, u=CH)
                idx_v = indices[st].rearrange("p (k u) -> p k u", u=CH)
                ea_v = eaT.rearrange("c (k n) -> c k n", k=NCH)
                sp.wait_ge(table_ready, st + 1)
                if kind == "weighted":
                    w = 256 if C == 32 else 128
                    sp.wait_ge(y_taken, NT * (st - 5))
                    sp.dma_start(tables[st].rearrange("(p t r) c -> p (t r c)", t=NT, r=REL),
                                 ysb[:, :, 0:w].rearrange("p t c -> p t c")).then_inc(table_written, 16)
                elif C == 32:
                    sp.dma_start(tables[st].rearrange("(p t) c -> p t c", t=NT), feat[:, :, 0:32]).then_inc(table_written, 16)
                else:
                    sp.dma_start(tables[st].rearrange("(p t) c -> p t c", t=NT),
                                 (nodes if st else feat)[:, :, 0:16]).then_inc(table_written, 16)
                m, _ = PICK.get(name, (0, 0))
                D = CH - m
                if m:
                    sp.wait_ge(table_written, 16 * (st + 1))
                    full = N // P
                    tf = table_f.rearrange("p a b -> p (a b)")[:, 0:FAR * NEAR * C].rearrange("p (b c) -> p b c", c=C)
                    sp.dma_start(tf[:, 0:full, :], tables[st][0:full * P, :].rearrange("(b p) c -> p b c", p=P))\
                        .then_inc(table_back, 16)
                    sp.dma_start(tf[0:N - full * P, full, :], tables[st][full * P:N, :]).then_inc(table_back, 16)
                ib = [16 * (HALF + 1) * st, 16 * HALF * st]
                gb = gather_base(st)
                pick_v = pick_index.rearrange("(a k n) -> a k n", a=1, k=NCH)
                h2_v = h2_dram.rearrange("c (k n) -> c k n", k=NCH)

                def store(k, s):
                    sp.wait_ge(rows_scanned, NCH * st + k + 1)
                    sp.dma_start(sums_v[:, k, :], scanned_rows[s][:, 0:CH * C // 32, :].rearrange("p a b -> p (a b)"))\
                        .then_inc(stored[s], 16)

                def body(k, s):
                    if not isinstance(k, int) or k >= 2:
                        sp.wait_ge(gathered[s], half(k) * (16 * D) + gb[s])
                    elif st:
                        sp.wait_ge(gathered[s], gb[s])
                    sp.dma_start(index[:, s, :], idx_v[:, k, :]).then_inc(index_loaded[s], 16)
                    more = m and (not known(k) or k + 1 < NCH)
                    if more and (not known(k) or st or k >= 1):
                        sp.wait_ge(hot_made, k * NEAR + NEAR * NCH * st)
                    if st == 0 and (not known(k) or k >= 2):
                        sp.wait_ge(h1_ready, k * PAIRS - PAIRS)
                    if kind == "mlp":
                        if not known(k) or k >= 2:
                            sp.wait_ge(w_ready, k * PAIRS + (NCH * PAIRS * (st - 2) - PAIRS))
                        elif st > 2:
                            sp.wait_ge(w_ready, NCH * PAIRS * (st - 2))
                        elif k == 0:
                            sp.wait_ge(h2_stored[0], 16 * (HALF + 1))
                            sp.wait_ge(h2_stored[1], 16 * HALF)
                    if more:
                        load_pick(k + 1, 1 - s)
                    if st == 0:
                        sp.dma_start(eaTs[s], ea_v[:, k, :]).then_inc(ea_loaded[s], 16)
                    if kind == "mlp":
                        sp.dma_start(h2s[s], h2_v[:, k, :]).then_inc(h2_loaded[s], 16)
                    if not isinstance(k, int) or k >= 2:
                        store(k - 2, s)

                if st:
                    sp.wait_ge(agg_gathered, 16 * NT * st)
                def load_pick(k, s):
                    sp.dma_start(pick_in[s][:, 0:m * P], pick_v[:, k, D * P:CH * P].broadcast_to([P, m * P]))\
                        .then_inc(pick_loaded[s], 16)

                if m:
                    if st:
                        sp.wait_ge(hot_made, NEAR * NCH * st)
                    load_pick(0, 0)
                over_chunks(sp, body)
                store(NCH - 2, 1)
                store(NCH - 1, 0)

            sp.wait_ge(table_ready, 9)
            sp.dma_start(table16.rearrange("(p t) c -> p t c", t=NT), X[:, :, :]).then_inc(table_written, 16)
            for half_, (w, b) in enumerate(((Wa, ba), (Wm, bm))):
                sp.dma_start(Wcat[0:16, half_, :], w).then_inc(Wcat_loaded, 16)
                sp.dma_start(Wcat[16:17, half_, :], b.rearrange("(a n) -> a n", a=1)).then_inc(Wcat_loaded, 16)
            sp.wait_ge(zeros_made, 1)
            for t in range(NT):
                sp.dma_start(attn_table[t * NP:(t + 1) * NP, :], zeros).then_inc(zeroed, 16)
            src3 = src.rearrange("p (k u) -> p k u", u=J3)
            neg3 = neg_flags.rearrange("p (k u) -> p k u", u=J3)
            ef3 = efT.rearrange("c (k n) -> c k n", k=N3)

            def load3(k, s):
                before = not known(k) or k >= 2
                if before:
                    sp.wait_ge(x_gathered[s], half(k) * (16 * J3))
                sp.dma_start(index[:, s, 0:J3], src3[:, k, :]).then_inc(index3_loaded[s], 16)
                if before:
                    sp.wait_ge(found, k * J3 - J3)
                sp.dma_start(neg_in[s], neg3[:, k, :]).then_inc(L3_loaded[s], 16)
                if before:
                    sp.wait_ge(wa_ready, k * J3 - J3)
                sp.dma_start(efTs[s], ef3[:, k, :]).then_inc(L3_loaded[s], 16)

            over_chunks3(sp, load3)
            sp.wait_ge(tail_scatter, 16)
            sp.dma_start(node_att, attn_table.rearrange("(p t) c -> p t c", t=NT)[:, :, CC:3 * CC]).then_inc(tail_dma, 16)
            sp.wait_ge(out_done, 1)
            sp.dma_start(out.rearrange("(p t) c -> p t c", t=NT), X[:, :, :]).then_inc(tail_dma, 16)
            sp.wait_ge(tail_dma, 32)

        @block.gpsimd
        def _(pool):
            nc.gpsimd.iota(iota_n, [[1, N + 1]], base=0, channel_multiplier=0).then_inc(pre_pool, 1)
            nc.gpsimd.iota(part_i, [[0, 1]], base=0, channel_multiplier=1).then_inc(pre_pool, 1)
            nc.gpsimd.iota(want_i, [[1, NT + 1]], base=0, channel_multiplier=NT).then_inc(pre_pool, 1)
            nc.gpsimd.memset(ident[:, :], 0.0).then_inc(pre_pool, 1)
            pool.wait_ge(pre_pool, 4)
            nc.gpsimd.affine_select(out=ident[:, :], in_=ident[:, :], compare_op=ALU.not_equal, fill=1.0, base=0,
                                    pattern=[[-1, P]], channel_multiplier=1).then_inc(pre_pool, 1)
            pool.wait_ge(rowno_made, 1)
            pool.wait_ge(pre_dma, 16 * 9)
            for t in range(NT + 1):
                if t >= 2:
                    pool.wait_ge(pre_pe2, t - 1)
                nc.gpsimd.indirect_dma_start(edge_rows[t % 2][:, :], None, dst_rows,
                                             bass.IndirectOffsetOnAxis(rowno[:, t:t + 1], 0)).then_inc(pre_gather[t % 2], 16)

            def paced_before(st):
                return 1 + (NCH - 5) * sum(2 if kind == "mlp" else 1 for _, _, kind in STAGES[:st])

            for st, (name, C, kind) in enumerate(STAGES):
                ib = [16 * (HALF + 1) * st, 16 * HALF * st]
                pool.wait_ge(table_written, 16 * (st + 1))

                def body(k, s):
                    pool.wait_ge(index_loaded[s], half(k) * 16 + (ib[s] + 16))
                    D = CH - PICK.get(name, (0, 0))[0]
                    first_part = D // 4 * 2
                    parts = [(0, first_part), (first_part, D)] if kind == "mlp" else [(0, D)]
                    for n, (u0, u1) in enumerate(parts):
                        if not known(k) or k >= 2:
                            if kind == "mlp":
                                pool.wait_ge(prod_done, k * PAIRS + (NCH * PAIRS * (st - 2) - 2 * PAIRS + u1 // 2))
                            else:
                                pool.wait_ge(rows_taken, k + (NCH * (st if st < 2 else st - DEPTH) - 1))
                        if not known(k):
                            pool.wait_ge(paced, k * len(parts) + (paced_before(st) - 2 * len(parts) + n))
                            nc.gpsimd.tensor_tensor(pace[0:1, 0:1], pace[0:1, 1:2], pace[0:1, 1:2], ALU.add).then_inc(paced, 1)
                        for u in range(u0, u1):
                            r = rows[s].rearrange("p a b -> p (a b)")
                            nc.gpsimd.indirect_dma_start(r[:, u * C:(u + 1) * C], None, tables[st],
                                                         bass.IndirectOffsetOnAxis(index[:, s, u:u + 1], 0))\
                                .then_inc(gathered[s], 16)

                over_chunks(pool, body)
                pool.wait_ge(stored[0], 16 * (HALF + 1) * (st + 1))
                pool.wait_ge(stored[1], 16 * HALF * (st + 1))
                aggf = agg.rearrange("p a b -> p (a b)")
                if st == 0:
                    pool.wait_ge(h1_ready, NCH * PAIRS)
                for t in range(NT):
                    nc.gpsimd.indirect_dma_start(aggf[:, t * C:(t + 1) * C], None, sums16 if C == 16 else sums32,
                                                 bass.IndirectOffsetOnAxis(last_edge[:, t:t + 1], 0)).then_inc(agg_gathered, 16)

            pool.wait_ge(table_written, 16 * 9)
            paced0 = paced_before(len(STAGES))

            def gather3(k, s):
                for u in range(J3):
                    nc.gpsimd.indirect_dma_start(xrows[s][:, u * 16:(u + 1) * 16], None, table16,
                                                 bass.IndirectOffsetOnAxis(index[:, s, u:u + 1], 0)).then_inc(x_gathered[s], 16)

            def scatter3(s):
                for u in range(J3):
                    nc.gpsimd.indirect_dma_start(attn_table, bass.IndirectOffsetOnAxis(end_of[:, s, u:u + 1], 0),
                                                 end_rows[:, u, :], None, bounds_check=N - 1, oob_is_err=False)\
                        .then_inc(scattered, 16)

            for k in range(2):
                pool.wait_ge(index3_loaded[k], 16)
                gather3(k, k)
            pool.wait_ge(zeroed, 16 * NT)

            def body3(k, s):
                if not known(k) or k + 2 < N3:
                    pool.wait_ge(scored, k * J3 + J3)
                    pool.wait_ge(index3_loaded[s], half(k) * 16 + 32)
                    if not known(k):
                        pool.wait_ge(paced, k * 2 + (paced0 - 4))
                        nc.gpsimd.tensor_tensor(pace[0:1, 0:1], pace[0:1, 1:2], pace[0:1, 1:2], ALU.add).then_inc(paced, 1)
                    gather3(k + 2, s)
                if not known(k) or k >= 1:
                    pool.wait_ge(end_loaded[1 - s], half(k + 1) * 16)
                    pool.wait_ge(rows_made, k * 3)
                    if not known(k):
                        pool.wait_ge(paced, k * 2 + (paced0 - 3))
                        nc.gpsimd.tensor_tensor(pace[0:1, 0:1], pace[0:1, 1:2], pace[0:1, 1:2], ALU.add).then_inc(paced, 1)
                    scatter3(1 - s)

            over_chunks3(pool, body3)
            pool.wait_ge(end_loaded[1], 16 * (N3 // 2))
            pool.wait_ge(rows_made, 3 * N3)
            scatter3(1)
            pool.wait_ge(scattered, 16 * J3 * N3)
            pool.wait_ge(own_cleared, 1)
            nc.gpsimd.indirect_dma_start(own, None, attn_table, bass.IndirectOffsetOnAxis(fix_index[:, :], 0),
                                         bounds_check=N - 1, oob_is_err=False).then_inc(tail_gather, 16)
            pool.wait_ge(fixed, 1)
            nc.gpsimd.indirect_dma_start(attn_table, bass.IndirectOffsetOnAxis(fix_index[:, :], 0), both, None,
                                         bounds_check=N - 1, oob_is_err=False).then_inc(tail_scatter, 16)

        @block.scalar
        def _(act):
            def dense_copies(d):
                cin = DENSE[d][0]
                for g in range(NG):
                    n = min(GROUP, NT - g * GROUP) * NP
                    act.wait_ge(transposed, NG * d + g + 1)
                    if d and g == 0:
                        act.wait_ge(dense_done, d)
                    nc.scalar.activation(featT[0:cin, g * GROUP * NP:g * GROUP * NP + n], ps[0:cin, g % 2, 0:n],
                                         ACT.Copy).then_inc(featT_ready, 1)

            def sqrt(n):
                act.wait_ge(to_sqrt, n)
                nc.scalar.activation(stat[:, 3, :], stat[:, 2, :], ACT.Sqrt).then_inc(sqrt_done, 1)

            sqrt(1)

            def hots(st, k, s):
                name = STAGES[st][0]
                m, groups = PICK[name]
                gb_ = groups_before(st)
                act.wait_ge(pick_loaded[s], half(k) * 16 + (16 * ((HALF + 1) if s == 0 else HALF) * st + 16))
                act.wait_ge(picked, (k * groups + (gb_ - groups)) if not known(k) or k >= 2 else gb_)
                for near in range(NEAR + 1):
                    if near < NEAR:
                        act.wait_ge(hot_made, k * NEAR + (NEAR * NCH * st + max(near - 1, 0)))
                        nc.scalar.activation(far_off[near % 2][:, 0:m * P], pick_in[s][:, 0:m * P], ACT.Abs,
                                             bias=neg_lanes[:, near:near + 1]).then_inc(off_made, 1)
                    if near:
                        act.wait_ge(off_made, k * NEAR + (NEAR * NCH * (st - 2) + near))
                        nc.scalar.activation(hot[s][:, near - 1, 0:m * P], far_off[(near - 1) % 2][:, 0:m * P], ACT.Relu,
                                             bias=1.0, scale=-1.0).then_inc(hot_made, 1)

            def make_h1(q, s, i):
                slot = ring(H_RING, s, i)
                act.wait_ge(h1_ready, q + 1)
                b = ago(H_RING, s, i)
                if not known(q) or q >= b:
                    act.wait_ge(h2_ready, q + (1 - b))
                nc.scalar.activation(h1s[slot], ps[:, H1_BANKS[slot], 0:2 * P], ACT.Gelu_apprx_tanh, bias=kb1s[:, 0:1])\
                    .then_inc(h1_made, 1)

            def make_h2(q, s, i):
                act.wait_ge(h2_ready, q + 1)
                slot, place = ring(H_RING, s, i), (i % PAIRS) * 2 * P
                nc.scalar.activation(h2s[s if i >= 0 else 1 - s][:, place:place + 2 * P], ps[:, H2_BANKS[slot], 0:2 * P],
                                     ACT.Gelu_apprx_tanh, bias=kb2s[:, 0:1]).then_inc(h2_made, 1)

            def store_h2(k, s):
                act.wait_ge(h2_made, k * PAIRS + PAIRS)
                act.dma_start(h2_dram.rearrange("c (k n) -> c k n", k=NCH)[:, k, :], h2s[s]).then_inc(h2_stored[s], 16)

            def mlp(k, s):
                for i in range(PAIRS):
                    q = k * PAIRS + i
                    make_h1(q, s, i)
                    if not (known(k) and q < 2):
                        make_h2(k * PAIRS + (i - 2), s, i - 2)
                    if i == 1 and (not known(k) or k >= 1):
                        store_h2(k - 1, 1 - s)
                    if i == 1 and (not known(k) or k >= 2):
                        act.wait_ge(h2_stored[s], half(k) * 16)

            over_chunks(act, mlp)
            make_h2(NCH * PAIRS - 2, 0, PAIRS - 2)
            make_h2(NCH * PAIRS - 1, 0, PAIRS - 1)
            store_h2(NCH - 1, 0)
            dense_copies(0)
            dense_copies(1)
            dense_copies(2)
            sqrt(2)
            for d in range(DEPTH):
                dense_copies(3 + d)
                st = 2 + d

                def chunk(k, s):
                    if not known(k) or k + 2 < NCH:
                        hots(st, k + 2, s)
                    o = scanned_rows[s].rearrange("p a b -> p (a b)")[:, 0:CH * 16].rearrange("p (u c) -> p u c", c=16)
                    so = scan_out.rearrange("p a b -> p (a b)")[:, 0:16 * (CH + 1)].rearrange("p (c u) -> p c u", u=CH + 1)
                    act.wait_ge(scanned, k + (NCH * st + 1))
                    act.wait_ge(stored[s], half(k) * 16 + 16 * ((HALF + 1) if s == 0 else HALF) * st)
                    nc.scalar.activation(o, so[:, :, 1:CH + 1].rearrange("p c u -> p u c"), ACT.Copy).then_inc(rows_scanned, 1)

                act.wait_ge(lanes_made, 1)
                hots(st, 0, 0)
                hots(st, 1, 1)
                over_chunks(act, chunk)
                act.wait_ge(to_gelu, d + 1)
                nc.scalar.activation(nodes[:, :, :], tmp[:, :, 0:16], ACT.Gelu_apprx_tanh).then_inc(gelu_done, 1)
            sqrt(3)
            for n, d in enumerate((7, 8)):
                dense_copies(d)
                w = REL_W[d][1]
                for t in range(NT):
                    act.wait_ge(y_ready, NT * n + t + 1)
                    nc.scalar.activation(ysb[:, t, 0:w], ps[0:NP, 2 + t % 2, 0:w], ACT.Copy).then_inc(y_taken, 1)
            sqrt(4)
            n3 = attn_neg.rearrange("p (c u) -> p c u", u=J3 + 1)
            p3 = [a.rearrange("p (c u) -> p c u", u=J3 + 1) for a in peak]
            d3 = decay.rearrange("p (c u) -> p c u", u=J3 + 1)
            e3 = [scores[s][:, 0, :].rearrange("p (c u) -> p c u", u=J3 + 1) for s in range(2)]
            t3 = [scores[s][:, 1, :].rearrange("p (c u) -> p c u", u=J3 + 1) for s in range(2)]

            end3 = end_index.rearrange("p (k u) -> p k u", u=J3)

            def make_neg(k, s):
                act.wait_ge(L3_loaded[s], half(k) * 32 + 32)
                nc.scalar.activation(n3[:, :, 1:J3 + 1], neg_in[s].unsqueeze(1).broadcast_to([P, CC, J3]), ACT.Copy)\
                    .then_inc(neg_made, 1)

            def rows_out(k, s):
                if not known(k) or k >= 1:
                    act.wait_ge(scattered, k * (16 * J3))
                nc.scalar.dma_start(end_of[:, s, :], end3[:, k, :]).then_inc(end_loaded[s], 16)
                for n, (a, ready) in enumerate(((p3[s], peaked), (e3[s], den_done), (t3[s], num_done))):
                    act.wait_ge(ready, k + 1)
                    nc.scalar.activation(end_rows[:, :, n * CC:(n + 1) * CC],
                                         a[:, :, 1:J3 + 1].rearrange("p c u -> p u c"), ACT.Copy).then_inc(rows_made, 1)

            def body3(k, s):
                act.wait_ge(peaked, k + 1)
                act.wait_ge(neg_made, k + 1)
                for u in range(J3):
                    nc.scalar.activation(n3[:, :, u + 1:u + 2], p3[s][:, :, u:u + 1], ACT.Identity,
                                         bias=neg_in[s][:, u:u + 1]).then_inc(found, 1)
                if not known(k) or k >= 1:
                    rows_out(k - 1, 1 - s)
                act.wait_ge(risen, k + 1)
                nc.scalar.activation(d3[:, :, 1:J3 + 1], e3[s][:, :, 1:J3 + 1], ACT.Relu).then_inc(clipped, 1)
                act.wait_ge(clipped, k * 2 + 1)
                nc.scalar.activation(e3[s][:, :, 1:J3 + 1], e3[s][:, :, 1:J3 + 1], ACT.Relu, scale=-1.0).then_inc(clipped, 1)
                if not known(k) or k + 1 < N3:
                    make_neg(k + 1, 1 - s)
                act.wait_ge(clipped, k * 2 + 2)
                nc.scalar.activation(e3[s][:, :, 1:J3 + 1], e3[s][:, :, 1:J3 + 1], ACT.Exp, scale=-1.0).then_inc(risen_exp, 1)
                nc.scalar.activation(d3[:, :, 1:J3 + 1], d3[:, :, 1:J3 + 1], ACT.Exp, scale=-1.0).then_inc(decay_exp, 1)

            act.wait_ge(zeros_made, 1)
            make_neg(0, 0)
            over_chunks3(act, body3)
            rows_out(N3 - 1, 1)
            act.wait_ge(tail_dve, 1)
            nc.scalar.activation(riseT, riseT, ACT.Exp).then_inc(tail_act, 1)
            act.wait_ge(tail_dve, 2)
            nc.scalar.activation(decT, decT, ACT.Exp).then_inc(tail_act, 1)
            act.wait_ge(tail_dve, 3)
            nc.scalar.activation(ea_, ea_, ACT.Exp).then_inc(tail_act, 1)
            act.wait_ge(tail_dve, 4)
            nc.scalar.activation(eb_, eb_, ACT.Exp).then_inc(tail_act, 1)
            sqrt(5)

        @block.tensor
        def _(pe):
            pe.wait_ge(loaded, 16 * len(LOADS))
            pe.wait_ge(pre_pool, 5)
            pe.wait_ge(below_made, 1)
            for t in range(NT + 1):
                m = nc.tensor.matmul(ps[0:NP, 6, t:t + 1], hits_n[:, t:t + NT * (NP - 1) + 1:NT], ones1, start=True, stop=True)
            m.then_inc(pre_pe, 1)
            pe.wait_ge(ends_counted, 1)
            nc.tensor.matmul(ps[:, 7, 0:REL], intake, lastf[:, 0, :], start=True, stop=True)
            nc.tensor.matmul(ps[:, 7, REL:2 * REL], intake2, lastf[:, 1, :], start=True, stop=True).then_inc(pre_pe, 1)

            def dense(d):
                cin, products = DENSE[d]
                src_t = feat if d < 3 or d == 8 else (nodes if d < 7 else X)
                pe.wait_ge(feat_ready, d + 1)
                for g in range(NG):
                    if NG * d + g >= 2:
                        pe.wait_ge(featT_ready, NG * d + g - 1)
                    for j in range(min(GROUP, NT - g * GROUP)):
                        m = nc.tensor.transpose(ps[0:cin, g % 2, j * NP:(j + 1) * NP],
                                                src_t[:, g * GROUP + j, 0:cin], ident[0:NP, 0:NP])
                    m.then_inc(transposed, 1)
                pe.wait_ge(featT_ready, NG * (d + 1))
                for W, width, bank in products:
                    for t in range(NT):
                        m = nc.tensor.matmul(dense_out(bank, width, t), featT[0:cin, t * NP:(t + 1) * NP], W,
                                             start=True, stop=True)
                m.then_inc(dense_done, 1)
                if d in REL_W:
                    n = d - 7
                    W, width = REL_W[d]
                    for t in range(NT):
                        if NT * n + t >= 2:
                            pe.wait_ge(y_taken, NT * n + t - 1)
                        nc.tensor.matmul(ps[0:NP, 2 + t % 2, 0:width], featT[0:cin, t * NP:(t + 1) * NP], W,
                                         start=True, stop=True).then_inc(y_ready, 1)

            def picks(st, k, s):
                name, C, kind = STAGES[st]
                m, groups = PICK[name]
                calls = []

                def tile(g, per, bank, t):
                    def go():
                        if g == 0 and t == 0:
                            pe.wait_ge(hot_made, k * NEAR + (NEAR * NCH * st + NEAR))
                        if t == 0:
                            before = groups_before(st) + g + 1 - groups
                            if not known(k) or k * groups + before > 0:
                                pe.wait_ge(masked, k * groups + before)
                        to = ps[:, bank, t * FAR * C:(t + 1) * FAR * C]
                        c = g * per + t
                        for near in range(NEAR):
                            for q in range(3):
                                part = table_p[q].rearrange("p a b -> p (a b)")[:, 0:FAR * NEAR * C]\
                                    .rearrange("p (n x) -> p n x", n=NEAR)
                                mm = nc.tensor.matmul(to, hot[s][:, near, c * P:(c + 1) * P], part[:, near, :],
                                                      start=(near == 0 and q == 0), stop=(near == NEAR - 1 and q == 2))
                        if t == per - 1:
                            mm.then_inc(picked, 1)
                    return go

                for g, c0, per, bank in pick_groups(st):
                    for t in range(per):
                        calls.append(tile(g, per, bank, t))
                return calls

            def start_picks(st):
                pe.wait_ge(parts_made, 3 * st + 3)
                for tile in picks(st, 0, 0):
                    tile()

            def span_sums(st, C):
                pe.wait_ge(rows_scanned, NCH * (st + 1))
                last = scanned_rows[0].rearrange("p a b -> p (a b)")[:, (CH - 1) * C:CH * C]
                for t in range(NT):
                    m = nc.tensor.matmul(dense_out(span_bank(C), C, t), spans[:, t:t + NT * (NP - 1) + 1:NT], last,
                                         start=True, stop=True)
                m.then_inc(spans_summed, 1)

            for st, (name, C, kind) in enumerate(STAGES):
                if kind == "mlp":
                    d = st - 2
                    dense(3 + d)
                    q0 = NCH * PAIRS * d

                    def third(q, b, s, i):
                        before = ago(W_RING, s, i)
                        if not known(q) or q0 + q >= before:
                            pe.wait_ge(prod_done, q + (q0 + 1 - before))
                        nc.tensor.matmul(ps[:, b, :], ones3[:, :], kb3w[:, :, :].rearrange("p a b -> p (a b)"),
                                         start=True, stop=False, skip_group_check=True)
                        for j in range(2):
                            m = nc.tensor.matmul(ps[:, b, j * CC:(j + 1) * CC], h2s[s][:, (2 * i + j) * P:(2 * i + j + 1) * P], kW3s[:, :],
                                                 start=False, stop=(j == 1), skip_group_check=True)
                        m.then_inc(w_ready, 1)

                    start_picks(st)

                    def body(k, s):
                        lb = [16 * (HALF + 1) * d, 16 * HALF * d]
                        pe.wait_ge(h2_loaded[s], half(k) * 16 + (lb[s] + 16))
                        tiles = picks(st, k + 1, 1 - s) if not known(k) or k + 1 < NCH else []
                        for i in range(PAIRS):
                            third(k * PAIRS + i, W_BANKS[ring(W_RING, s, i)], s, i)
                            if 2 <= i < 2 + len(tiles):
                                tiles[i - 2]()

                    over_chunks(pe, body)
                if st == 0:
                    start_picks(st)

                    def first(q, s, i):
                        b = ago(H_RING, s, i)
                        if not known(q) or q >= b:
                            pe.wait_ge(h1_made, q + (1 - b))
                        nc.tensor.matmul(ps[:, H1_BANKS[ring(H_RING, s, i)], 0:2 * P], kW1s[:, :],
                                         eaTs[s][:, i * 2 * P:(i + 1) * 2 * P], start=True, stop=True).then_inc(h1_ready, 1)

                    def second(q, s, i):
                        slot, b = ring(H_RING, s, i), ago(H_RING, s, i)
                        pe.wait_ge(h1_made, q + 1)
                        if not known(q) or q >= b:
                            pe.wait_ge(h2_made, q + (1 - b))
                        nc.tensor.matmul(ps[:, H2_BANKS[slot], 0:2 * P], kW2s[:, :], h1s[slot], start=True, stop=True)\
                            .then_inc(h2_ready, 1)

                    def body0(k, s):
                        pe.wait_ge(ea_loaded[s], half(k) * 16 + 16)
                        tiles = picks(0, k + 1, 1 - s) if not known(k) or k + 1 < NCH else []
                        for i in range(PAIRS):
                            q = k * PAIRS + i
                            first(q, s, i)
                            if i >= PAIRS - len(tiles):
                                tiles[i - (PAIRS - len(tiles))]()
                            if not (known(k) and q < 2):
                                second(k * PAIRS + (i - 2), s, i - 2)

                    over_chunks(pe, body0)
                    second(NCH * PAIRS - 2, 0, PAIRS - 2)
                    second(NCH * PAIRS - 1, 0, PAIRS - 1)
                if st == 1:
                    start_picks(st)

                    def body1(k, s):
                        if not known(k) or k + 1 < NCH:
                            for tile in picks(1, k + 1, 1 - s):
                                tile()

                    over_chunks(pe, body1)
                if kind == "weighted":
                    dense(st + 1)
                span_sums(st, C)
                if st == 0:
                    dense(0)
                    dense(1)
                if st == 1:
                    dense(2)

            pe.wait_ge(Wcat_loaded, 64)
            pe.wait_ge(tail_ready, 1)
            RING = 8

            def body3(k, s):
                pe.wait_ge(L3_loaded[s], half(k) * 32 + 32)
                for u in range(J3):
                    back_ = RING if u >= RING else (J3 - RING if u < J3 - RING else J3)
                    if not known(k) or k * J3 + u - back_ >= 0:
                        pe.wait_ge(scored, k * J3 + (u - back_ + 1))
                    nc.tensor.matmul(ps[:, u % RING, :], efTs[s][:, u * P:(u + 1) * P],
                                     Wcat.rearrange("p a b -> p (a b)"), start=True, stop=True).then_inc(wa_ready, 1)

            over_chunks3(pe, body3)
            pe.wait_ge(num_done, N3)
            pe.wait_ge(scored, N3 * J3)
            u = J3 + 1
            pe.wait_ge(peaked, N3)
            for h in range(2):
                pk = peak[1].rearrange("p (c u) -> p c u", u=u)[:, h * P:(h + 1) * P, J3]
                nc.tensor.transpose(ps[:, 0, h * P:(h + 1) * P], pk, ident[:, :])
                for q in range(2):
                    st_ = scores[1][:, q, :].rearrange("p (c u) -> p c u", u=u)[:, h * P:(h + 1) * P, J3]
                    m = nc.tensor.transpose(ps[:, 1 + q, h * P:(h + 1) * P], st_, ident[:, :])
            m.then_inc(tail_pe, 1)
            pe.wait_ge(shift_made, 1)
            for q in range(3):
                for h in range(2):
                    m = nc.tensor.transpose(ps[:, 3 + q, h * P:(h + 1) * P], shiftT[:, q, h * (P + 1):h * (P + 1) + P], ident[:, :])
            m.then_inc(tail_pe, 1)

        @block.vector
        def _(dve):
            v = nc.vector
            n_made = [0]

            def step(ins):
                ins.then_inc(made, 1)
                n_made[0] += 1
                dve.wait_ge(made, n_made[0])

            v.memset(nexti, -1).then_inc(nexti_cleared, 1)
            v.memset(pace[:, :], 0.0).then_inc(paced, 1)
            step(v.memset(ones3[:, :], 1.0))
            step(v.memset(ones1, 1.0))
            dve.wait_ge(loaded, 16 * len(LOADS))
            step(v.tensor_copy(kb3p[:, 0, :], kb3s[:, :]))
            step(v.tensor_tensor(kb3r[:, 0, :], kb3s[:, :], kb3p[:, 0, :], ALU.subtract))
            step(v.tensor_copy(kb3p[:, 1, :], kb3r[:, 0, :]))
            step(v.tensor_tensor(kb3r[:, 1, :], kb3r[:, 0, :], kb3p[:, 1, :], ALU.subtract))
            v.tensor_copy(kb3p[:, 2, :], kb3r[:, 1, :]).then_inc(kb3_split, 1)
            v.tensor_copy(dstf, dsti).then_inc(dstf_made, 1)
            dve.wait_ge(dstf_made, 1)
            step(v.tensor_copy(colfirst, dstf[:, 0:1]))
            step(v.tensor_copy(collast, dstf[:, COLS - 1:COLS]))
            dve.wait_ge(pre_pool, 5)
            step(v.tensor_copy(node_row, iota_n))
            v.tensor_scalar(hits_n, node_row, collast, None, ALU.is_gt).then_inc(below_made, 1)
            step(v.tensor_copy(typef, typei))
            step(v.tensor_copy(total, srci))
            step(v.tensor_copy(srcTf, srcTi))
            step(v.memset(pick_mask[:, :, :], 0.0))
            step(v.tensor_scalar(far, total, float(BLOCK), None, ALU.is_ge))
            for i in range(2, FAR):
                step(v.scalar_tensor_tensor(out=far, in0=total, scalar=float(BLOCK * i), in1=far, op0=ALU.is_ge, op1=ALU.add))
            for i in range(FAR):
                step(v.tensor_scalar(pick_mask[:, :, i], far, float(i), None, ALU.is_equal))
            step(v.tensor_scalar(far, srcTf, float(BLOCK), None, ALU.is_ge))
            for i in range(2, FAR):
                step(v.scalar_tensor_tensor(out=far, in0=srcTf, scalar=float(BLOCK * i), in1=far, op0=ALU.is_ge, op1=ALU.add))
            v.scalar_tensor_tensor(out=pick_f16, in0=far, scalar=-float(BLOCK), in1=srcTf, op0=ALU.mult, op1=ALU.add)\
                .then_inc(pickidx_made, 1)
            step(v.scalar_tensor_tensor(out=idxf, in0=total, scalar=float(REL), in1=typef, op0=ALU.mult, op1=ALU.add))
            v.tensor_copy(srci, idxf).then_inc(relidx_made, 1)
            step(v.tensor_copy(want, want_i))
            dve.wait_ge(pre_pe, 1)
            step(v.tensor_copy(rowno_f, ps[0:NP, 6, 0:NT + 1]))
            v.tensor_copy(rowno, rowno_f).then_inc(rowno_made, 1)
            for t in range(NT + 1):
                dve.wait_ge(pre_gather[t % 2], 16 * (t // 2 + 1))
                if t:
                    dve.wait_ge(pre_pe2, t)
                v.tensor_scalar(hits, edge_rows[t % 2], want[:, t:t + 1], 0.0, ALU.is_lt, ALU.add,
                                accum_out=lower[:, t:t + 1]).then_inc(pre_pe2, 1)
            dve.wait_ge(pre_pe2, NT + 1)
            step(v.scalar_tensor_tensor(out=lower, in0=rowno_f, scalar=float(COLS), in1=lower, op0=ALU.mult, op1=ALU.add))
            step(v.tensor_tensor(deg[:, :], lower[:, 1:NT + 1], lower[:, 0:NT], ALU.subtract))
            step(v.tensor_scalar(nodeq, lower[:, 1:NT + 1], -1.0, 0.0, ALU.add, ALU.max))
            step(v.tensor_copy(last_edge[:, :], nodeq))
            step(v.tensor_scalar(has[:, :], deg[:, :], 0.0, None, ALU.is_gt))
            step(v.tensor_scalar(nodeq2, deg[:, :], 1.0, None, ALU.max))
            step(v.reciprocal(nodeq3, nodeq2))
            step(v.tensor_tensor(inv_deg[:, :], nodeq3, has[:, :], ALU.mult))
            step(v.memset(notstart[:, 0:1], 0.0))
            step(v.tensor_tensor(notstart[:, 1:COLS], dstf[:, 1:COLS], dstf[:, 0:COLS - 1], ALU.is_equal))
            step(v.memset(nextsame[:, COLS - 1:COLS], 0.0))
            step(v.tensor_tensor(nextsame[:, 0:COLS - 1], dstf[:, 1:COLS], dstf[:, 0:COLS - 1], ALU.is_equal))
            dve.wait_ge(pre_dma, 16 * 9)
            step(v.tensor_copy(nextfirst, nexti))
            step(v.tensor_tensor(spaneq, collast, nextfirst, ALU.is_equal))
            step(v.scalar_tensor_tensor(out=spanval, in0=collast, scalar=1.0, in1=spaneq, op0=ALU.add, op1=ALU.mult))
            step(v.tensor_scalar(spanneg, spanval, -1.0, None, ALU.add))
            step(v.tensor_scalar(spans[:, :], node_row[:, 0:N], spanneg, None, ALU.is_equal))
            step(v.tensor_copy(endf, nextsame))
            step(v.tensor_copy(endf[:, COLS - 1:COLS], spaneq))
            step(v.scalar_tensor_tensor(out=endf, in0=endf, scalar=float(SKIP), in1=dstf, op0=ALU.mult, op1=ALU.add))
            v.tensor_copy(endi, endf).then_inc(endidx_made, 1)
            v.tensor_scalar(negf, notstart[:, :], -1.0, BIG, ALU.add, ALU.mult).then_inc(negf_made, 1)
            step(v.tensor_copy(partno, part_i))
            for i in range(NEAR):
                step(v.tensor_scalar(lanes[:, i:i + 1], partno, float(P * i), None, ALU.add))
            v.tensor_scalar(neg_lanes[:, :], lanes[:, :], -1.0, None, ALU.mult).then_inc(lanes_made, 1)
            step(v.tensor_copy(firstrow, firstrow_i))
            step(v.tensor_copy(lastrow, lastrow_i))
            step(v.tensor_tensor(wholerow, firstrow, lastrow, ALU.is_equal))
            step(v.memset(prevlast_row[:, 0:1], 0.0))
            step(v.tensor_tensor(prevlast_row[:, 1:P], lastrow[:, 0:P - 1], firstrow[:, 1:P], ALU.is_equal))
            step(v.tensor_tensor(wholerow, wholerow, prevlast_row, ALU.mult))
            step(v.tensor_scalar(chain[:, :], wholerow, -1.0, BIG, ALU.add, ALU.mult))
            step(v.tensor_scalar(wholerow, node_row[:, 0:P], partno, None, ALU.is_equal))
            step(v.tensor_tensor(wholerow, wholerow, prevlast_row, ALU.mult))
            step(v.tensor_reduce(small[:, 8:9], wholerow, AX_X, ALU.add))
            step(v.tensor_tensor(small[:, 9:10], colfirst, collast, ALU.is_equal))
            step(v.tensor_tensor(small[:, 10:11], small[:, 9:10], spaneq, ALU.mult))
            step(v.tensor_scalar(small[:, 11:12], small[:, 10:11], -1.0, 1.0, ALU.mult, ALU.add))
            step(v.tensor_tensor(small[:, 12:13], small[:, 11:12], small[:, 8:9], ALU.mult))
            step(v.tensor_scalar(small[:, 13:14], small[:, 12:13], -float(SKIP), float(SKIP), ALU.mult, ALU.add))
            step(v.tensor_tensor(small[:, 14:15], small[:, 13:14], colfirst, ALU.add))
            step(v.tensor_copy(fix_index[:, :], small[:, 14:15]))
            step(v.tensor_scalar(colno, node_row[:, 0:P], partno, None, ALU.is_gt))
            step(v.tensor_scalar(firstrow, firstrow, collast, None, ALU.is_equal))
            step(v.tensor_tensor(intake, firstrow, colno, ALU.mult))
            step(v.tensor_scalar(colno, node_row[:, 0:P], partno, None, ALU.is_lt))
            step(v.tensor_scalar(lastrow, lastrow, colfirst, None, ALU.is_equal))
            step(v.tensor_tensor(intake2, lastrow, colno, ALU.mult))
            step(v.tensor_scalar(isfirst, dstf, colfirst, None, ALU.is_equal))
            step(v.tensor_scalar(islast, dstf, collast, None, ALU.is_equal))
            for r in range(REL):
                step(v.tensor_scalar(relf[r], typef, float(r), None, ALU.is_equal))
                step(v.tensor_tensor_scan(relsum[r], notstart[:, :], relf[r], 0.0, ALU.mult, ALU.add))
                step(v.tensor_tensor_scan(back[:, ::-1], nextsame[:, ::-1], relf[r][:, ::-1], 0.0, ALU.mult, ALU.add))
                step(v.tensor_copy(lastf[:, 0, r:r + 1], relsum[r][:, COLS - 1:COLS]))
                step(v.tensor_copy(lastf[:, 1, r:r + 1], back[:, 0:1]))
                step(v.tensor_tensor(relsum[r], relsum[r], back, ALU.add))
            v.memset(weight[:, :], 0.0).then_inc(ends_counted, 1)
            dve.wait_ge(ends_counted, 1)
            dve.wait_ge(pre_pe, 2)
            step(v.tensor_copy(inout.rearrange("p a b -> p (a b)"), ps[:, 7, 0:2 * REL]))
            for r in range(REL):
                step(v.scalar_tensor_tensor(out=back, in0=isfirst, scalar=inout[:, 0, r:r + 1], in1=relsum[r],
                                            op0=ALU.mult, op1=ALU.add))
                step(v.scalar_tensor_tensor(out=total, in0=islast, scalar=inout[:, 1, r:r + 1], in1=back,
                                            op0=ALU.mult, op1=ALU.add))
                step(v.scalar_tensor_tensor(out=back, in0=total, scalar=-1.0, in1=relf[r], op0=ALU.add, op1=ALU.mult))
                step(v.tensor_tensor(weight[:, :], weight[:, :], back, ALU.add))
            step(v.tensor_scalar(weight[:, :], weight[:, :], 1.0, None, ALU.max))
            step(v.reciprocal(weight[:, :], weight[:, :]))
            dve.wait_ge(pre_dma, 16 * 12)

            def over_t(a, c):
                return a.unsqueeze(2).broadcast_to([NP, NT, c])

            def over_c(b, n, c):
                return b.unsqueeze(1).broadcast_to([NP, n, c])

            n_sqrt = [0]

            def root(from_):
                from_.then_inc(to_sqrt, 1)
                n_sqrt[0] += 1
                dve.wait_ge(sqrt_done, n_sqrt[0])
                step(v.reciprocal(stat[:, 1, :], stat[:, 3, :]))

            def layernorm(y, square=None):
                sq = tmp[:, :, 32:48] if square is None else square
                step(v.tensor_reduce(stat[:, 0, :], y, AX_X, ALU.add))
                step(v.tensor_scalar(stat[:, 0, :], stat[:, 0, :], 1.0 / 16, None, ALU.mult))
                step(v.tensor_tensor(y, y, over_t(stat[:, 0, :], 16), ALU.subtract))
                step(v.tensor_tensor(sq, y, y, ALU.mult))
                step(v.tensor_reduce(stat[:, 0, :], sq, AX_X, ALU.add))
                root(v.tensor_scalar(stat[:, 2, :], stat[:, 0, :], 1.0 / 16, EPS, ALU.mult, ALU.add))
                step(v.tensor_tensor(X[:, :, :], y, over_t(stat[:, 1, :], 16), ALU.mult))

            def flat(C, a):
                return a.rearrange("p a b -> p (a b)")[:, 0:NT * C].rearrange("p (t c) -> p t c", c=C)

            def finish_sums(st, C):
                a = flat(C, agg)
                dve.wait_ge(agg_gathered, 16 * NT * (st + 1))
                step(v.tensor_tensor(a, a, over_t(has[:, :], C), ALU.mult))
                dve.wait_ge(spans_summed, st + 1)
                for t0, n, piece in dense_all(6, C):
                    step(v.tensor_tensor(a[:, t0:t0 + n, :], a[:, t0:t0 + n, :], piece, ALU.add))
                return a

            def add_dense(d, y, bank, width, other=None):
                dve.wait_ge(dense_done, d + 1)
                for t0, n, piece in dense_all(bank, width):
                    step(v.tensor_tensor(y[:, t0:t0 + n, :], (y if other is None else other)[:, t0:t0 + n, :], piece, ALU.add))

            def edge_sums(st, C, kind):
                taken = st if st < 2 else st - DEPTH
                sin = scan_in.rearrange("p a b -> p (a b)")[:, 0:C * (CH + 1)]
                sfl = scan_flag.rearrange("p a b -> p (a b)")[:, 0:C * (CH + 1)]
                sout = scan_out.rearrange("p a b -> p (a b)")[:, 0:C * (CH + 1)]
                sin3, sfl3, sout3 = (a.rearrange("p (c u) -> p c u", u=CH + 1) for a in (sin, sfl, sout))
                q0 = NCH * PAIRS * (st - 2)
                k0 = NCH * st
                name = STAGES[st][0]
                m, groups = PICK.get(name, (0, 0))
                D = CH - m
                gb = gather_base(st)

                def make_hot(k, s):
                    if kind == "mlp":
                        return
                    dve.wait_ge(pick_loaded[s], half(k) * 16 + (16 * ((HALF + 1) if s == 0 else HALF) * st + 16))
                    if not known(k) or k >= 2 or st:
                        dve.wait_ge(picked, k * groups + (groups_before(st) - (groups if (not known(k) or k >= 2) else k * groups)))
                    for near in range(NEAR):
                        v.tensor_scalar(hot[s][:, near, 0:m * P], pick_in[s][:, 0:m * P], lanes[:, near:near + 1], None,
                                        ALU.is_equal).then_inc(hot_made, 1)

                def keep(k, s):
                    r = rows[s].rearrange("p a b -> p (a b)")[:, 0:CH * C].rearrange("p (u c) -> p u c", c=C)
                    mask = pick_mask[:, :, :].rearrange("p (k u) f -> p k u f", u=CH)
                    gb_ = groups_before(st)
                    all_groups = pick_groups(st)
                    for g in range(groups + 1):
                        if g < groups:
                            _, c0, per, bank = all_groups[g]
                            dve.wait_ge(picked, k * groups + (gb_ + g + 1))
                            if not known(k) or k * groups + gb_ + g >= 2:
                                dve.wait_ge(kept_rows, k * groups + (gb_ + g - 1))
                            v.tensor_tensor(kept[g % 2][:, 0:per * FAR * C].rearrange("p (u f c) -> p u f c", u=per, f=FAR),
                                            ps[:, bank, 0:per * FAR * C].rearrange("p (u f c) -> p u f c", u=per, f=FAR),
                                            mask[:, k, c0:c0 + per, :].unsqueeze(3).broadcast_to([P, per, FAR, C]),
                                            ALU.mult).then_inc(masked, 1)
                        if g:
                            _, c0, per, _ = all_groups[g - 1]
                            dve.wait_ge(masked, k * groups + (gb_ + g))
                            v.tensor_reduce(r[:, c0:c0 + per, :],
                                            kept[(g - 1) % 2][:, 0:per * FAR * C].rearrange("p (u f c) -> p u c f", u=per, f=FAR),
                                            AX_X, ALU.add).then_inc(kept_rows, 1)

                if m:
                    dve.wait_ge(table_back, 32 * (st + 1))
                    tf, tr = (a.rearrange("p a b -> p (a b)")[:, 0:FAR * NEAR * C].rearrange("p (f n c) -> p n f c", n=NEAR, c=C)
                              for a in (table_f, table_r))
                    tp = [a.rearrange("p a b -> p (a b)")[:, 0:FAR * NEAR * C].rearrange("p (n f c) -> p n f c", n=NEAR, c=C)
                          for a in table_p]
                    def part(q, frm):
                        for near in range(NEAR):
                            i_ = v.tensor_copy(tp[q][:, near], frm[:, near])
                            if near < NEAR - 1:
                                step(i_)
                        i_.then_inc(parts_made, 1)
                        dve.wait_ge(parts_made, 3 * st + q + 1)
                    def rest(q, frm):
                        for near in range(NEAR):
                            step(v.tensor_tensor(tr[:, near], frm[:, near], tp[q][:, near], ALU.subtract))
                    part(0, tf)
                    rest(0, tf)
                    part(1, tr)
                    rest(1, tr)
                    part(2, tr)
                    make_hot(0, 0)
                    make_hot(1, 1)
                step(v.memset(sfl3[:, :, 0:1], 0.0))
                v.memset(sin3[:, :, 0:1], 0.0).then_inc(carried, 1)

                def body(k, s):
                    r = rows[s].rearrange("p a b -> p (a b)")[:, 0:CH * C].rearrange("p (u c) -> p u c", c=C)
                    o = scanned_rows[s].rearrange("p a b -> p (a b)")[:, 0:CH * C].rearrange("p (u c) -> p u c", c=C)
                    flags = notstart[:, :].rearrange("p (k u) -> p k u", u=CH)[:, k, :]
                    if not isinstance(k, int) or k0 + k >= 1:
                        dve.wait_ge(scanned, k + k0)
                    v.tensor_scalar(sfl3[:, :, 1:CH + 1], flags.unsqueeze(1).broadcast_to([P, C, CH]), 1.0, None,
                                    ALU.mult).then_inc(flags_made, 1)
                    if kind == "mlp":
                        dve.wait_ge(gathered[s], half(k) * (16 * D) + (gb[s] + 16 * D))
                        if m:
                            dve.wait_ge(kept_rows, k * groups + (groups_before(st) + groups))
                        for i in range(PAIRS + 1):
                            if i < PAIRS:
                                q = k * PAIRS + i
                                dve.wait_ge(w_ready, q + (q0 + 1))
                                if i >= 3:
                                    dve.wait_ge(reduced, q + (q0 - 2))
                                v.tensor_tensor(prod[i % 3].rearrange("p t (i o) -> p t i o", i=16),
                                                ps[:, W_BANKS[ring(W_RING, s, i)], :].rearrange("p (t i o) -> p t i o", t=2, i=16),
                                                r[:, 2 * i:2 * i + 2, :].unsqueeze(3).broadcast_to([P, 2, 16, 16]),
                                                ALU.mult).then_inc(prod_done, 1)
                            if i:
                                q = k * PAIRS + i - 1
                                dve.wait_ge(prod_done, q + (q0 + 1))
                                v.tensor_reduce(sin3[:, :, 2 * i - 1:2 * i + 1].rearrange("p o t -> p t o"),
                                                prod[(i - 1) % 3].rearrange("p t (i o) -> p t o i", i=16), AX_X, ALU.add)\
                                    .then_inc(reduced, 1)
                        if not known(k) or k + 1 < NCH:
                            keep(k + 1, 1 - s)
                        dve.wait_ge(reduced, k * PAIRS + (q0 + PAIRS))
                    else:
                        dve.wait_ge(gathered[s], half(k) * (16 * D) + (gb[s] + 16 * D))
                        if m:
                            dve.wait_ge(kept_rows, k * groups + (groups_before(st) + groups))
                        to = sin3[:, :, 1:CH + 1].rearrange("p c u -> p u c")
                        if kind == "weighted":
                            w = weight[:, :].rearrange("p (k u) -> p k u", u=CH)[:, k, :]
                            v.tensor_tensor(to, r, w.unsqueeze(2).broadcast_to([P, CH, C]), ALU.mult).then_inc(rows_taken, 1)
                        else:
                            v.tensor_copy(to, r).then_inc(rows_taken, 1)
                        dve.wait_ge(rows_taken, k + (NCH * taken + 1))
                    dve.wait_ge(flags_made, k + (k0 + 1))
                    dve.wait_ge(carried, k + (k0 + st + 1))
                    if not isinstance(k, int) or k0 + k >= 1:
                        dve.wait_ge(rows_scanned, k + k0)
                    v.tensor_tensor_scan(sout, sfl, sin, 0.0, ALU.mult, ALU.add).then_inc(scanned, 1)
                    dve.wait_ge(scanned, k + (k0 + 1))
                    v.tensor_copy(sin3[:, :, 0:1], sout3[:, :, CH:CH + 1]).then_inc(carried, 1)
                    if kind == "mlp":
                        return
                    sb0 = 16 * ((HALF + 1) if s == 0 else HALF) * st
                    if not isinstance(k, int) or k >= 2 or st:
                        dve.wait_ge(stored[s], half(k) * 16 + sb0)
                    v.tensor_copy(o, sout3[:, :, 1:CH + 1].rearrange("p c u -> p u c")).then_inc(rows_scanned, 1)

                def chunk(k, s):
                    if m and (not known(k) or k + 2 < NCH):
                        make_hot(k + 2, s)
                    body(k, s)
                    if m and kind != "mlp" and (not known(k) or k + 1 < NCH):
                        keep(k + 1, 1 - s)

                if m:
                    keep(0, 0)
                over_chunks(dve, chunk)
                dve.wait_ge(carried, k0 + NCH + st + 1)

            step(v.memset(table_f.rearrange("p a b -> p (a b)"), 0.0))
            root(v.tensor_scalar(stat[:, 2, :], deg[:, :], 1.0, None, ALU.add))
            step(v.tensor_copy(dinv[:, :], stat[:, 1, :]))
            f16 = feat[:, :, 0:16]
            v.tensor_tensor(f16, X[:, :, :], over_t(dinv[:, :], 16), ALU.mult).then_inc(table_ready, 1)
            edge_sums(0, 16, "plain")
            a = finish_sums(0, 16)
            step(v.tensor_tensor(a, a, f16, ALU.add))
            dve.wait_ge(table_written, 16)
            v.tensor_tensor(f16, a, over_t(dinv[:, :], 16), ALU.mult).then_inc(feat_ready, 1)
            add_dense(0, tmp[:, :, 0:48], 2, 48, other=b1s[:, :].unsqueeze(1).broadcast_to([NP, NT, 48]))
            v.tensor_scalar(feat[:, :, 0:48], tmp[:, :, 0:48], 0.0, None, ALU.max).then_inc(feat_ready, 1)
            dve.wait_ge(dense_done, 2)
            f32_ = feat[:, :, 0:32]
            for t0, n, piece in dense_all(2, 32):
                m = v.tensor_tensor(f32_[:, t0:t0 + n, :], piece, over_t(dinv[:, :], 32)[:, t0:t0 + n, :], ALU.mult)
                if t0 + n < NT:
                    step(m)
            m.then_inc(table_ready, 1)
            edge_sums(1, 32, "plain")
            a = finish_sums(1, 32)
            step(v.tensor_tensor(a, a, f32_, ALU.add))
            step(v.tensor_tensor(a, a, over_t(dinv[:, :], 32), ALU.mult))
            step(v.tensor_tensor(a, a, over_c(b2s[:, :], NT, 32), ALU.add))
            dve.wait_ge(table_written, 32)
            v.tensor_scalar(f32_, a, 0.0, None, ALU.max).then_inc(feat_ready, 1)
            add_dense(2, tmp[:, :, 0:16], 2, 16, other=over_c(bfcs[:, :], NT, 16))
            step(v.tensor_tensor(tmp[:, :, 0:16], tmp[:, :, 0:16], X[:, :, :], ALU.add))
            layernorm(tmp[:, :, 0:16])
            step(v.tensor_copy(nodes[:, :, :], X[:, :, :]))
            for d in range(DEPTH):
                st = 2 + d
                step(v.memset(stat[:, 0, :], 0.0))
                v.memset(stat[:, 1, :], 0.0).then_inc(table_ready, 1)
                v.memset(stat[:, 2, :], 0.0).then_inc(feat_ready, 1)
                edge_sums(st, 16, "mlp")
                a = finish_sums(st, 16)
                step(v.tensor_tensor(a, a, over_t(inv_deg[:, :], 16), ALU.mult))
                step(v.tensor_tensor(a, a, over_c(rootbs[:, d, :], NT, 16), ALU.add))
                dve.wait_ge(dense_done, 4 + d)
                dve.wait_ge(table_written, 16 * (st + 1))
                v.tensor_tensor(tmp[:, :, 0:16], a, ps[0:NP, 7, 0:NT * 16].rearrange("p (t c) -> p t c", c=16),
                                ALU.add).then_inc(to_gelu, 1)
                dve.wait_ge(gelu_done, d + 1)
            step(v.tensor_tensor(tmp[:, :, 0:16], nodes[:, :, :], X[:, :, :], ALU.add))
            layernorm(tmp[:, :, 0:16])
            step(v.memset(stat[:, 0, :], 0.0))
            v.memset(stat[:, 1, :], 0.0).then_inc(table_ready, 1)
            v.memset(stat[:, 2, :], 0.0).then_inc(feat_ready, 1)
            edge_sums(6, 32, "weighted")
            a = finish_sums(6, 32)
            step(v.tensor_tensor(a, a, over_c(Rb1s[:, :], NT, 32), ALU.add))
            add_dense(7, a, 4, 32)
            dve.wait_ge(table_written, 16 * 7)
            step(v.tensor_scalar(feat[:, :, 0:32], a, 0.0, None, ALU.max))
            v.memset(stat[:, 1, :], 0.0).then_inc(table_ready, 1)
            v.memset(stat[:, 2, :], 0.0).then_inc(feat_ready, 1)
            edge_sums(7, 16, "weighted")
            a = finish_sums(7, 16)
            step(v.tensor_tensor(a, a, over_c(Rb2s[:, :], NT, 16), ALU.add))
            add_dense(8, a, 4, 16)
            step(v.tensor_tensor(tmp[:, :, 0:16], a, X[:, :, :], ALU.add))
            layernorm(tmp[:, :, 0:16])
            U = J3 + 1
            n3, d3 = (a.rearrange("p (c u) -> p c u", u=U) for a in (attn_neg, decay))
            p3 = [a.rearrange("p (c u) -> p c u", u=U) for a in peak]
            e3 = [scores[s][:, 0, :].rearrange("p (c u) -> p c u", u=U) for s in range(2)]
            t3 = [scores[s][:, 1, :].rearrange("p (c u) -> p c u", u=U) for s in range(2)]
            step(v.memset(n3[:, :, 0:1], -BIG))
            step(v.memset(d3[:, :, 0:1], 0.0))
            step(v.memset(p3[1][:, :, J3:U], 0.0))
            step(v.memset(e3[1][:, :, J3:U], 0.0))
            step(v.memset(t3[1][:, :, J3:U], 0.0))
            step(v.tensor_copy(nodes[:, :, :], X[:, :, :]))
            step(v.memset(zeros, 0.0))
            v.memset(stat[:, 0, :], 0.0).then_inc(zeros_made, 1)
            v.memset(stat[:, 1, :], 0.0).then_inc(tail_ready, 1)
            v.memset(stat[:, 2, :], 0.0).then_inc(table_ready, 1)

            def score(k, s):
                dve.wait_ge(x_gathered[s], half(k) * (16 * J3) + 16 * J3)
                if not known(k) or k >= 2:
                    dve.wait_ge(rows_made, k * 3 - 3)
                for u in range(J3):
                    dve.wait_ge(wa_ready, k * J3 + (u + 1))
                    to = scores[s].rearrange("p a (i o u) -> p a i o u", i=16, o=16)[:, :, :, :, u + 1]
                    x_ = xrows[s][:, u * 16:(u + 1) * 16].unsqueeze(1).unsqueeze(3).broadcast_to([P, 2, 16, 16])
                    v.tensor_tensor(to, ps[:, u % 8, :].rearrange("p (a i o) -> p a i o", a=2, i=16), x_,
                                    ALU.mult).then_inc(scored, 1)

            def attend(k, s):
                v.tensor_copy(e3[s][:, :, 0:1], p3[1 - s][:, :, J3:U]).then_inc(carries, 1)
                dve.wait_ge(carries, k * 3 + 1)
                dve.wait_ge(scored, k * J3 + J3)
                dve.wait_ge(neg_made, k + 1)
                v.tensor_tensor_scan(peak[s], attn_neg, scores[s][:, 0, :], 0.0, ALU.add, ALU.max).then_inc(peaked, 1)
                if not known(k) or k >= 1:
                    sums(k - 1, 1 - s)
                dve.wait_ge(peaked, k + 1)
                v.tensor_copy(e3[s][:, :, 0:1], e3[1 - s][:, :, J3:U]).then_inc(carries, 1)
                v.tensor_copy(t3[s][:, :, 0:1], t3[1 - s][:, :, J3:U]).then_inc(carries, 1)
                dve.wait_ge(found, k * J3 + J3)
                v.tensor_tensor(e3[s][:, :, 1:U], e3[s][:, :, 1:U], n3[:, :, 1:U], ALU.subtract).then_inc(risen, 1)
                dve.wait_ge(carries, k * 3 + 3)
                if not known(k) or k + 1 < N3:
                    score(k + 1, 1 - s)

            def sums(k, s):
                dve.wait_ge(risen_exp, k + 1)
                v.tensor_tensor(t3[s][:, :, 1:U], t3[s][:, :, 1:U], e3[s][:, :, 1:U], ALU.mult).then_inc(weighted_msg, 1)
                dve.wait_ge(weighted_msg, k + 1)
                dve.wait_ge(decay_exp, k + 1)
                v.tensor_tensor_scan(scores[s][:, 0, :], decay, scores[s][:, 0, :], 0.0, ALU.mult, ALU.add).then_inc(den_done, 1)
                v.tensor_tensor_scan(scores[s][:, 1, :], decay, scores[s][:, 1, :], 0.0, ALU.mult, ALU.add).then_inc(num_done, 1)
                dve.wait_ge(den_done, k + 1)
                dve.wait_ge(num_done, k + 1)

            score(0, 0)
            over_chunks3(dve, attend)
            sums(N3 - 1, 1)
            dve.wait_ge(rows_made, 3 * N3)
            dve.wait_ge(tail_pe, 1)
            for q in range(3):
                step(v.tensor_copy(lastT[:, q, :], ps[:, q, 0:2 * P]))
            step(v.tensor_copy(chainT.rearrange("p (a b) -> p a b", a=2), chain[:, :].unsqueeze(1).broadcast_to([P, 2, P])))
            step(v.tensor_tensor_scan(peakT, chainT, lastT[:, 0, :], 0.0, ALU.add, ALU.max))
            v.tensor_tensor(riseT, lastT[:, 0, :], peakT, ALU.subtract).then_inc(tail_dve, 1)
            step(v.memset(decT, -BIG))
            cT, kT, xT = (a.rearrange("p (a b) -> p a b", a=2) for a in (chainT, peakT, decT))
            step(v.tensor_tensor(xT[:, :, 1:P], cT[:, :, 1:P], kT[:, :, 0:P - 1], ALU.add))
            v.tensor_tensor(xT[:, :, 1:P], xT[:, :, 1:P], kT[:, :, 1:P], ALU.subtract).then_inc(tail_dve, 1)
            dve.wait_ge(tail_act, 2)
            step(v.tensor_tensor(denT, lastT[:, 1, :], riseT, ALU.mult))
            step(v.tensor_tensor(numT, lastT[:, 2, :], riseT, ALU.mult))
            step(v.tensor_tensor_scan(lastT[:, 1, :], decT, denT, 0.0, ALU.mult, ALU.add))
            step(v.tensor_tensor_scan(lastT[:, 2, :], decT, numT, 0.0, ALU.mult, ALU.add))
            step(v.memset(shiftT, 0.0))
            for q, a in enumerate((peakT, lastT[:, 1, :], lastT[:, 2, :])):
                step(v.tensor_copy(shiftT[:, q, :].rearrange("p (a b) -> p a b", a=2)[:, :, 1:P + 1],
                                   a.rearrange("p (a b) -> p a b", a=2)))
            v.memset(own, 0.0).then_inc(own_cleared, 1)
            v.memset(both, 0.0).then_inc(shift_made, 1)
            dve.wait_ge(tail_gather, 16)
            dve.wait_ge(tail_pe, 2)
            for q in range(3):
                step(v.tensor_copy(cin[:, q, :], ps[:, 3 + q, 0:2 * P]))
            step(v.tensor_tensor(both[:, 0:CC], own[:, 0:CC], cin[:, 0, :], ALU.max))
            v.tensor_tensor(ea_, own[:, 0:CC], both[:, 0:CC], ALU.subtract).then_inc(tail_dve, 1)
            v.tensor_tensor(eb_, cin[:, 0, :], both[:, 0:CC], ALU.subtract).then_inc(tail_dve, 1)
            dve.wait_ge(tail_act, 4)
            for q in (1, 2):
                o_ = own[:, q * CC:(q + 1) * CC]
                step(v.tensor_tensor(o_, o_, ea_, ALU.mult))
                step(v.tensor_tensor(cin[:, q, :], cin[:, q, :], eb_, ALU.mult))
                step(v.tensor_tensor(both[:, q * CC:(q + 1) * CC], o_, cin[:, q, :], ALU.add))
            v.memset(stat3[:, :], 0.0).then_inc(fixed, 1)
            dve.wait_ge(tail_dma, 16)
            step(v.tensor_scalar(nohas, has[:, :], -1.0, 1.0, ALU.mult, ALU.add))
            den, num = node_att[:, :, 0:CC], node_att[:, :, CC:2 * CC]
            step(v.tensor_tensor(den, den, over_t(nohas, CC), ALU.add))
            step(v.reciprocal(den, den))
            step(v.tensor_tensor(num, num, den, ALU.mult))
            step(v.tensor_reduce(summed, num.rearrange("p t (i o) -> p t o i", i=16), AX_X, ALU.add))
            step(v.tensor_tensor(summed, summed, nodes[:, :, :], ALU.add))
            layernorm(summed, summed2)
            v.memset(stat3[:, :], 0.0).then_inc(out_done, 1)


_INS = ["x", "src", "srcT", "dst", "dst_ends", "edge_type_8", "eaT", "efT", "L0_gnn_W1", "L0_gnn_b1", "L0_gnn_W2", "L0_gnn_b2",
        "L0_gnn_Wfc", "L0_gnn_bfc", "L1_gnn_kW1", "L1_gnn_kb1", "L1_gnn_kW2", "L1_gnn_kb2", "L1_gnn_kW3",
        "L1_gnn_kb3", "L1_gnn_root_W", "L1_gnn_root_b", "L2_gnn_W1", "L2_gnn_root1", "L2_gnn_b1", "L2_gnn_W2",
        "L2_gnn_root2", "L2_gnn_b2", "L3_gnn_W_msg", "L3_gnn_b_msg", "L3_gnn_W_attn", "L3_gnn_b_attn"]


def kernel(**inputs):
    import numpy as _np
    import concourse.bacc as _bacc
    from concourse.bass_utils import run_bass_kernel_spmd as _run

    a = {k: _np.asarray(v) for k, v in inputs.items()}
    pad = P * COLS - E

    def edges(v, fill):
        tail = _np.full((pad,) + v.shape[1:], fill, v.dtype)
        return _np.concatenate([v, tail]).reshape((P, COLS) + v.shape[1:])

    a["src"], a["dst"], a["edge_type_8"] = edges(a["src"], 0), edges(a["dst"], N), edges(a["edge_type_8"], 0)
    a["srcT"] = _np.ascontiguousarray(a["src"].T).reshape(P, COLS)
    a["dst_ends"] = _np.stack([a["dst"][:, 0], a["dst"][:, -1]])
    a["eaT"] = edges(a["edge_attr_6"], 0).transpose(2, 1, 0).reshape(6, COLS * P)
    a["efT"] = edges(a["edge_attr_16"], 0).transpose(2, 1, 0).reshape(16, COLS * P)
    a["efT"] = _np.concatenate([a["efT"], _np.ones((1, COLS * P), a["efT"].dtype)])
    nc = _bacc.Bacc("TRN2", target_bir_lowering=False, num_devices=1)
    arrays, args = {}, []
    for name in _INS:
        v = _np.ascontiguousarray(a[name])
        arrays["in_" + name] = v
        args.append(nc.dram_tensor("in_" + name, v.shape, mybir.dt.from_np(v.dtype), kind="ExternalInput").ap())
    out = nc.dram_tensor("out_0", (N, LAT), F32, kind="ExternalOutput").ap()
    build(nc, *args, out)
    r = _run(nc, [arrays], core_ids=[0])
    return r.results[0]["out_0"]
```
